# Optimizing a Trainium2 kernel written in Bass

```python
import numpy as np
import jax
import jax.numpy as jnp

def _softmax(x, axis=-1):
    return jax.nn.softmax(x, axis=axis)

def _gelu(x):
    return jax.nn.gelu(x, approximate=True)

def _silu(x):
    return jax.nn.silu(x)

def _sigmoid(x):
    return jax.nn.sigmoid(x)

def _layernorm(x, axis=-1, eps=1e-05):
    m = jnp.mean(x, axis=axis, keepdims=True)
    v = jnp.var(x, axis=axis, keepdims=True)
    return (x - m) / jnp.sqrt(v + eps)

def _scatter_add(tgt, idx, src, axis=0):
    return tgt.at[idx].add(src)

def _segment_sum(src, seg, n):
    return jax.ops.segment_sum(src, seg, n)
kernel_name = 'mk_xattn_seq_d4_seqx_r8_3c2079'

def setup_inputs(seed: int=0):
    np.random.seed(seed)
    _w = jnp.asarray

    def _rec_inputs():
        import jax
        import jax.numpy as jnp
        _rk = jax.random.key(seed)
        x = -0.0002928 + 1 * jax.random.normal(jax.random.fold_in(_rk, 1), (8, 128, 256), jnp.float32)
        _lenS = 128 - jax.random.randint(jax.random.fold_in(_rk, 7), (8,), 0, max(1, 128 // 4) + 1, jnp.int32)
        _lenS2 = 128 - jax.random.randint(jax.random.fold_in(_rk, 8), (8,), 0, max(1, 128 // 4) + 1, jnp.int32)
        _ctx_2048P = jax.random.normal(jax.random.fold_in(_rk, 11), (8, 16, 256), jnp.float32)
        _ctx_2048c = jax.random.dirichlet(jax.random.fold_in(_rk, 511), 0.3 * jnp.ones((16,), jnp.float32), (8, 128))
        _ctx_2048t = jnp.einsum('bsk,bkd->bsd', _ctx_2048c, _ctx_2048P)
        _ctx_2048t = _ctx_2048t * jax.lax.rsqrt(jnp.mean(jnp.square(_ctx_2048t)) + 1e-12) * 0.953939
        ctx_2048 = -1.39393e-06 + 0.999914 * (_ctx_2048t + 0.3 * jax.random.normal(jax.random.fold_in(_rk, 611), (8, 128, 256), jnp.float32))
        _validS = jnp.arange(128)[None, :] < _lenS[:, None]
        _validS2 = jnp.arange(128)[None, :] < _lenS2[:, None]
        _causal = jnp.tril(jnp.ones((128, 128), dtype=bool))
        mask_Bx1xSxS2_ff0 = jnp.where(jnp.ones((8, 1, 128, 128), dtype=bool), 0.0, -1000000000.0).astype(jnp.float32)
        mask_1x1xSxS2_fc1 = jnp.where(jnp.broadcast_to(_validS2[0:1, None, None, :], (1, 1, 128, 128)), 1.0, 0.0).astype(jnp.float32)
        mask_Bx1xSxS2_ff1 = jnp.where(jnp.ones((8, 1, 128, 128), dtype=bool), 1.0, 0.0).astype(jnp.float32)
        return (x, ctx_2048, mask_Bx1xSxS2_ff0, mask_1x1xSxS2_fc1, mask_Bx1xSxS2_ff1)
    x, ctx_2048, mask_Bx1xSxS2_ff0, mask_1x1xSxS2_fc1, mask_Bx1xSxS2_ff1 = _rec_inputs()

    def _L0_xattn_setup():
        import jax, jax.numpy as jnp
        import numpy as np
        D_MODEL = 128
        N_HEAD = 16
        D_HEAD = 64
        IDX_LIST = [128, 256]
        SCALE = 1.0 / D_HEAD ** 0.5
        LN_EPS = 1e-05
        key = jax.random.key(seed)
        ks = jax.random.split(key, 9)
        s = 0.02
        B, L = (2, 256)
        return {'z1ss': jax.random.normal(ks[0], (B, D_MODEL, L), dtype=jnp.float32), 'u1ss': jax.random.normal(ks[1], (B, D_MODEL, L), dtype=jnp.float32), 'Wqkv0': jax.random.normal(ks[2], (3 * N_HEAD * D_HEAD, D_MODEL), dtype=jnp.float32) * s, 'Wqkv1': jax.random.normal(ks[3], (3 * N_HEAD * D_HEAD, D_MODEL), dtype=jnp.float32) * s, 'Winj0': jax.random.normal(ks[4], (3 * N_HEAD * D_HEAD, D_MODEL), dtype=jnp.float32) * s, 'Winj1': jax.random.normal(ks[5], (3 * N_HEAD * D_HEAD, D_MODEL), dtype=jnp.float32) * s, 'Wo': jax.random.normal(ks[6], (D_MODEL, N_HEAD * D_HEAD), dtype=jnp.float32) * s, 'bo': jax.random.normal(ks[7], (D_MODEL,), dtype=jnp.float32) * s, 'r_w_bias': jax.random.uniform(ks[8], (N_HEAD, D_HEAD), minval=-0.05, maxval=0.05, dtype=jnp.float32)}
    _L0_xattn_all = _L0_xattn_setup()
    _L0_xattn_in = {k: v for k, v in _L0_xattn_all.items() if k in ('Wqkv0', 'Wqkv1', 'Winj0', 'Winj1', 'Wo', 'bo', 'r_w_bias')}
    del _L0_xattn_all

    def _L1_xattn_setup():
        import jax, jax.numpy as jnp
        import numpy as np
        H = 256
        NH = 32
        KVH = 8
        HD = H // NH
        GROUPS = NH // KVH
        EPS = 1e-06
        B, L, S = (4, 128, 128)

        def _gqa_forward(hidden_state, encoder_hidden_state, encoder_attention_mask, Wq, bq, Wk, bk, Wv, bv, Wo, bo, gamma, beta):
            b, l, _ = hidden_state.shape
            s = encoder_hidden_state.shape[1]
            q = hidden_state @ Wq + bq
            k = encoder_hidden_state @ Wk + bk
            v = encoder_hidden_state @ Wv + bv
            q = q.reshape(b, l, KVH, GROUPS, HD).transpose(0, 2, 3, 1, 4)
            k = k.reshape(b, s, KVH, HD).transpose(0, 2, 1, 3)
            v = v.reshape(b, s, KVH, HD).transpose(0, 2, 1, 3)
            scale = 1.0 / jnp.sqrt(jnp.asarray(HD, q.dtype))
            scores = jnp.einsum('bkgld,bksd->bkgls', q, k) * scale
            scores = scores + encoder_attention_mask[:, :, None, :, :]
            attn = jax.nn.softmax(scores, axis=-1)
            out = jnp.einsum('bkgls,bksd->bkgld', attn, v)
            out = out.transpose(0, 3, 1, 2, 4).reshape(b, l, H)
            out = out @ Wo + bo
            x = out + hidden_state
            mu = jnp.mean(x, axis=-1, keepdims=True)
            var = jnp.var(x, axis=-1, keepdims=True)
            return (x - mu) * jax.lax.rsqrt(var + EPS) * gamma + beta
        key = jax.random.key(seed)
        ks = jax.random.split(key, 12)
        sd = 0.02
        return {'hidden_state': jax.random.normal(ks[0], (B, L, H), jnp.float32), 'encoder_hidden_state': jax.random.normal(ks[1], (B, S, H), jnp.float32), 'encoder_attention_mask': jnp.zeros((B, 1, L, S), jnp.float32), 'Wq': jax.random.normal(ks[2], (H, H), jnp.float32) * sd, 'bq': jnp.zeros((H,), jnp.float32), 'Wk': jax.random.normal(ks[3], (H, KVH * HD), jnp.float32) * sd, 'bk': jnp.zeros((KVH * HD,), jnp.float32), 'Wv': jax.random.normal(ks[4], (H, KVH * HD), jnp.float32) * sd, 'bv': jnp.zeros((KVH * HD,), jnp.float32), 'Wo': jax.random.normal(ks[5], (H, H), jnp.float32) * sd, 'bo': jnp.zeros((H,), jnp.float32), 'gamma': jnp.ones((H,), jnp.float32), 'beta': jnp.zeros((H,), jnp.float32)}
    _L1_xattn_all = _L1_xattn_setup()
    _L1_xattn_in = {k: v for k, v in _L1_xattn_all.items() if k in ('Wq', 'bq', 'Wk', 'bk', 'Wv', 'bv', 'Wo', 'bo', 'gamma', 'beta')}
    del _L1_xattn_all

    def _L2_xattn_setup():
        import jax, jax.numpy as jnp
        import numpy as np
        B, Q, S1, S2 = (4, 32, 256, 256)
        D, H, K, F = (256, 16, 128, 1024)
        LN_EPS = 1e-05

        def _layer_norm(x, scale, offset):
            mu = jnp.mean(x, axis=-1, keepdims=True)
            var = jnp.var(x, axis=-1, keepdims=True)
            return (x - mu) * jax.lax.rsqrt(var + LN_EPS) * scale + offset

        def _cross_attention(q_in, kv_in, wq, bq, wk, bk, wv, bv, wo, bo, bias_k, bias_v):
            b, q_len, _ = q_in.shape
            t = kv_in.shape[1]
            qh = (q_in @ wq + bq).reshape(b, q_len, H, K)
            kh = (kv_in @ wk + bk).reshape(b, t, H, K)
            vh = (kv_in @ wv + bv).reshape(b, t, H, K)
            kh = jnp.concatenate([kh, jnp.broadcast_to(bias_k, (b, 1, H, K))], axis=1)
            vh = jnp.concatenate([vh, jnp.broadcast_to(bias_v, (b, 1, H, K))], axis=1)
            scale = jnp.sqrt(jnp.asarray(K, q_in.dtype))
            logits = jnp.einsum('bqhk,bthk->bhqt', qh, kh) / scale
            weights = jax.nn.softmax(logits, axis=-1)
            ctx = jnp.einsum('bhqt,bthk->bqhk', weights, vh).reshape(b, q_len, H * K)
            return ctx @ wo + bo

        def _forward(x, xf_1, xf_2, ln1_scale, ln1_offset, wq1, bq1, wk1, bk1, wv1, bv1, wo1, bo1, bias_k1, bias_v1, ln2_scale, ln2_offset, wq2, bq2, wk2, bk2, wv2, bv2, wo2, bo2, bias_k2, bias_v2, ln_mlp_scale, ln_mlp_offset, w_fc1, b_fc1, w_fc2, b_fc2):
            res = x
            h = _layer_norm(x, ln1_scale, ln1_offset)
            x = res + _cross_attention(h, xf_1, wq1, bq1, wk1, bk1, wv1, bv1, wo1, bo1, bias_k1, bias_v1)
            res = x
            h = _layer_norm(x, ln2_scale, ln2_offset)
            x = res + _cross_attention(h, xf_2, wq2, bq2, wk2, bk2, wv2, bv2, wo2, bo2, bias_k2, bias_v2)
            h = _layer_norm(x, ln_mlp_scale, ln_mlp_offset)
            h = jax.nn.gelu(h @ w_fc1 + b_fc1, approximate=False) @ w_fc2 + b_fc2
            return x + h
        key = jax.random.key(seed)
        ks = iter(jax.random.split(key, 64))

        def rn(shape, s=0.02):
            return jax.random.normal(next(ks), shape, jnp.float32) * s
        inp = {'x': rn((B, Q, D), 1.0), 'xf_1': rn((B, S1, D), 1.0), 'xf_2': rn((B, S2, D), 1.0)}
        for i in (1, 2):
            inp[f'ln{i}_scale'] = jnp.ones((D,), jnp.float32)
            inp[f'ln{i}_offset'] = jnp.zeros((D,), jnp.float32)
            inp[f'wq{i}'] = rn((D, H * K))
            inp[f'bq{i}'] = jnp.zeros((H * K,), jnp.float32)
            inp[f'wk{i}'] = rn((D, H * K))
            inp[f'bk{i}'] = jnp.zeros((H * K,), jnp.float32)
            inp[f'wv{i}'] = rn((D, H * K))
            inp[f'bv{i}'] = jnp.zeros((H * K,), jnp.float32)
            inp[f'wo{i}'] = rn((H * K, D))
            inp[f'bo{i}'] = jnp.zeros((D,), jnp.float32)
            inp[f'bias_k{i}'] = rn((1, 1, H, K))
            inp[f'bias_v{i}'] = rn((1, 1, H, K))
        inp['ln_mlp_scale'] = jnp.ones((D,), jnp.float32)
        inp['ln_mlp_offset'] = jnp.zeros((D,), jnp.float32)
        inp['w_fc1'] = rn((D, F))
        inp['b_fc1'] = jnp.zeros((F,), jnp.float32)
        inp['w_fc2'] = rn((F, D))
        inp['b_fc2'] = jnp.zeros((D,), jnp.float32)
        return inp
    _L2_xattn_all = _L2_xattn_setup()
    _L2_xattn_in = {k: v for k, v in _L2_xattn_all.items() if k in ('ln1_scale', 'ln1_offset', 'wq1', 'bq1', 'wk1', 'bk1', 'wv1', 'bv1', 'wo1', 'bo1', 'bias_k1', 'bias_v1', 'ln2_scale', 'ln2_offset', 'wq2', 'bq2', 'wk2', 'bk2', 'wv2', 'bv2', 'wo2', 'bo2', 'bias_k2', 'bias_v2', 'ln_mlp_scale', 'ln_mlp_offset', 'w_fc1', 'b_fc1', 'w_fc2', 'b_fc2')}
    del _L2_xattn_all

    def _L3_xattn_setup():
        import jax, jax.numpy as jnp
        import numpy as np
        H = 256
        NH = 16
        HD = H // NH
        EPS = 1e-05

        def gelu(x):
            return 0.5 * x * (1.0 + jnp.tanh(0.7978845608028654 * x * (1.0 + 0.044715 * x * x)))

        def layernorm(x, scale, bias):
            m = jnp.mean(x, axis=-1, keepdims=True)
            v = jnp.mean(jnp.square(x - m), axis=-1, keepdims=True)
            return (x - m) * jax.lax.rsqrt(v + EPS) * scale + bias

        def split_heads(x):
            b, s, _ = x.shape
            return x.reshape(b, s, NH, HD).transpose(0, 2, 1, 3)

        def merge_heads(x):
            b, nh, s, hd = x.shape
            return x.transpose(0, 2, 1, 3).reshape(b, s, nh * hd)

        def attention(q, k, v, mask):
            scores = jnp.einsum('bhqd,bhkd->bhqk', q, k) / jnp.sqrt(jnp.float32(HD))
            scores = scores * mask - 10000.0 * (1.0 - mask)
            probs = jax.nn.softmax(scores, axis=-1)
            return jnp.einsum('bhqk,bhkd->bhqd', probs, v)
        key = jax.random.key(seed)
        ks = jax.random.split(key, 16)
        b, s, t = (2, 128, 128)
        w = lambda k, i, o: jax.random.normal(k, (i, o), jnp.float32) * 0.02
        inp = {'hidden_states': jax.random.normal(ks[0], (b, s, H), jnp.float32), 'encoder_states': jax.random.normal(ks[1], (b, t, H), jnp.float32), 'ltor_mask': jnp.tril(jnp.ones((1, 1, s, s), jnp.float32)), 'cross_mask': jnp.ones((b, 1, s, t), jnp.float32), 'ln1_s': jnp.ones((H,), jnp.float32), 'ln1_b': jnp.zeros((H,), jnp.float32), 'w_qkv': w(ks[2], H, 3 * H), 'b_qkv': jnp.zeros((3 * H,), jnp.float32), 'w_ao': w(ks[3], H, H), 'b_ao': jnp.zeros((H,), jnp.float32), 'ln2_s': jnp.ones((H,), jnp.float32), 'ln2_b': jnp.zeros((H,), jnp.float32), 'w_q': w(ks[4], H, H), 'b_q': jnp.zeros((H,), jnp.float32), 'w_kv': w(ks[5], H, 2 * H), 'b_kv': jnp.zeros((2 * H,), jnp.float32), 'w_co': w(ks[6], H, H), 'b_co': jnp.zeros((H,), jnp.float32), 'ln3_s': jnp.ones((H,), jnp.float32), 'ln3_b': jnp.zeros((H,), jnp.float32), 'w1': w(ks[7], H, 4 * H), 'b1': jnp.zeros((4 * H,), jnp.float32), 'w2': w(ks[8], 4 * H, H), 'b2': jnp.zeros((H,), jnp.float32)}
        return inp
    _L3_xattn_all = _L3_xattn_setup()
    _L3_xattn_in = {k: v for k, v in _L3_xattn_all.items() if k in ('ln1_s', 'ln1_b', 'w_qkv', 'b_qkv', 'w_ao', 'b_ao', 'ln2_s', 'ln2_b', 'w_q', 'b_q', 'w_kv', 'b_kv', 'w_co', 'b_co', 'ln3_s', 'ln3_b', 'w1', 'b1', 'w2', 'b2')}
    del _L3_xattn_all
    return {'x': x, 'ctx_2048': ctx_2048, 'mask_Bx1xSxS2_ff0': mask_Bx1xSxS2_ff0, 'mask_1x1xSxS2_fc1': mask_1x1xSxS2_fc1, 'mask_Bx1xSxS2_ff1': mask_Bx1xSxS2_ff1, 'L0_xattn_Wqkv0': _L0_xattn_in['Wqkv0'], 'L0_xattn_Wqkv1': _L0_xattn_in['Wqkv1'], 'L0_xattn_Winj0': _L0_xattn_in['Winj0'], 'L0_xattn_Winj1': _L0_xattn_in['Winj1'], 'L0_xattn_Wo': _L0_xattn_in['Wo'], 'L0_xattn_bo': _L0_xattn_in['bo'], 'L0_xattn_r_w_bias': _L0_xattn_in['r_w_bias'], 'L1_xattn_Wq': _L1_xattn_in['Wq'], 'L1_xattn_bq': _L1_xattn_in['bq'], 'L1_xattn_Wk': _L1_xattn_in['Wk'], 'L1_xattn_bk': _L1_xattn_in['bk'], 'L1_xattn_Wv': _L1_xattn_in['Wv'], 'L1_xattn_bv': _L1_xattn_in['bv'], 'L1_xattn_Wo': _L1_xattn_in['Wo'], 'L1_xattn_bo': _L1_xattn_in['bo'], 'L1_xattn_gamma': _L1_xattn_in['gamma'], 'L1_xattn_beta': _L1_xattn_in['beta'], 'L2_xattn_ln1_scale': _L2_xattn_in['ln1_scale'], 'L2_xattn_ln1_offset': _L2_xattn_in['ln1_offset'], 'L2_xattn_wq1': _L2_xattn_in['wq1'], 'L2_xattn_bq1': _L2_xattn_in['bq1'], 'L2_xattn_wk1': _L2_xattn_in['wk1'], 'L2_xattn_bk1': _L2_xattn_in['bk1'], 'L2_xattn_wv1': _L2_xattn_in['wv1'], 'L2_xattn_bv1': _L2_xattn_in['bv1'], 'L2_xattn_wo1': _L2_xattn_in['wo1'], 'L2_xattn_bo1': _L2_xattn_in['bo1'], 'L2_xattn_bias_k1': _L2_xattn_in['bias_k1'], 'L2_xattn_bias_v1': _L2_xattn_in['bias_v1'], 'L2_xattn_ln2_scale': _L2_xattn_in['ln2_scale'], 'L2_xattn_ln2_offset': _L2_xattn_in['ln2_offset'], 'L2_xattn_wq2': _L2_xattn_in['wq2'], 'L2_xattn_bq2': _L2_xattn_in['bq2'], 'L2_xattn_wk2': _L2_xattn_in['wk2'], 'L2_xattn_bk2': _L2_xattn_in['bk2'], 'L2_xattn_wv2': _L2_xattn_in['wv2'], 'L2_xattn_bv2': _L2_xattn_in['bv2'], 'L2_xattn_wo2': _L2_xattn_in['wo2'], 'L2_xattn_bo2': _L2_xattn_in['bo2'], 'L2_xattn_bias_k2': _L2_xattn_in['bias_k2'], 'L2_xattn_bias_v2': _L2_xattn_in['bias_v2'], 'L2_xattn_ln_mlp_scale': _L2_xattn_in['ln_mlp_scale'], 'L2_xattn_ln_mlp_offset': _L2_xattn_in['ln_mlp_offset'], 'L2_xattn_w_fc1': _L2_xattn_in['w_fc1'], 'L2_xattn_b_fc1': _L2_xattn_in['b_fc1'], 'L2_xattn_w_fc2': _L2_xattn_in['w_fc2'], 'L2_xattn_b_fc2': _L2_xattn_in['b_fc2'], 'L3_xattn_ln1_s': _L3_xattn_in['ln1_s'], 'L3_xattn_ln1_b': _L3_xattn_in['ln1_b'], 'L3_xattn_w_qkv': _L3_xattn_in['w_qkv'], 'L3_xattn_b_qkv': _L3_xattn_in['b_qkv'], 'L3_xattn_w_ao': _L3_xattn_in['w_ao'], 'L3_xattn_b_ao': _L3_xattn_in['b_ao'], 'L3_xattn_ln2_s': _L3_xattn_in['ln2_s'], 'L3_xattn_ln2_b': _L3_xattn_in['ln2_b'], 'L3_xattn_w_q': _L3_xattn_in['w_q'], 'L3_xattn_b_q': _L3_xattn_in['b_q'], 'L3_xattn_w_kv': _L3_xattn_in['w_kv'], 'L3_xattn_b_kv': _L3_xattn_in['b_kv'], 'L3_xattn_w_co': _L3_xattn_in['w_co'], 'L3_xattn_b_co': _L3_xattn_in['b_co'], 'L3_xattn_ln3_s': _L3_xattn_in['ln3_s'], 'L3_xattn_ln3_b': _L3_xattn_in['ln3_b'], 'L3_xattn_w1': _L3_xattn_in['w1'], 'L3_xattn_b1': _L3_xattn_in['b1'], 'L3_xattn_w2': _L3_xattn_in['w2'], 'L3_xattn_b2': _L3_xattn_in['b2']}

def reference(x, ctx_2048, mask_Bx1xSxS2_ff0, mask_1x1xSxS2_fc1, mask_Bx1xSxS2_ff1, L0_xattn_Wqkv0, L0_xattn_Wqkv1, L0_xattn_Winj0, L0_xattn_Winj1, L0_xattn_Wo, L0_xattn_bo, L0_xattn_r_w_bias, L1_xattn_Wq, L1_xattn_bq, L1_xattn_Wk, L1_xattn_bk, L1_xattn_Wv, L1_xattn_bv, L1_xattn_Wo, L1_xattn_bo, L1_xattn_gamma, L1_xattn_beta, L2_xattn_ln1_scale, L2_xattn_ln1_offset, L2_xattn_wq1, L2_xattn_bq1, L2_xattn_wk1, L2_xattn_bk1, L2_xattn_wv1, L2_xattn_bv1, L2_xattn_wo1, L2_xattn_bo1, L2_xattn_bias_k1, L2_xattn_bias_v1, L2_xattn_ln2_scale, L2_xattn_ln2_offset, L2_xattn_wq2, L2_xattn_bq2, L2_xattn_wk2, L2_xattn_bk2, L2_xattn_wv2, L2_xattn_bv2, L2_xattn_wo2, L2_xattn_bo2, L2_xattn_bias_k2, L2_xattn_bias_v2, L2_xattn_ln_mlp_scale, L2_xattn_ln_mlp_offset, L2_xattn_w_fc1, L2_xattn_b_fc1, L2_xattn_w_fc2, L2_xattn_b_fc2, L3_xattn_ln1_s, L3_xattn_ln1_b, L3_xattn_w_qkv, L3_xattn_b_qkv, L3_xattn_w_ao, L3_xattn_b_ao, L3_xattn_ln2_s, L3_xattn_ln2_b, L3_xattn_w_q, L3_xattn_b_q, L3_xattn_w_kv, L3_xattn_b_kv, L3_xattn_w_co, L3_xattn_b_co, L3_xattn_ln3_s, L3_xattn_ln3_b, L3_xattn_w1, L3_xattn_b1, L3_xattn_w2, L3_xattn_b2):
    import jax
    import jax.numpy as jnp

    def _L0_xattn_ref(z1ss, u1ss, Wqkv0, Wqkv1, Winj0, Winj1, Wo, bo, r_w_bias):
        import jax, jax.numpy as jnp
        import numpy as np
        D_MODEL = 128
        N_HEAD = 16
        D_HEAD = 64
        IDX_LIST = [128, 256]
        SCALE = 1.0 / D_HEAD ** 0.5
        LN_EPS = 1e-05
        bsz, d_model, qlen = z1ss.shape
        bounds = [0] + IDX_LIST
        Wq_list, Wi_list = ([Wqkv0, Wqkv1], [Winj0, Winj1])
        chunks = []
        for i in range(len(IDX_LIST)):
            s, e = (bounds[i], bounds[i + 1])
            h = jnp.einsum('od,bdl->bol', Wq_list[i], z1ss[:, :, s:e])
            h = h + jnp.einsum('od,bdl->bol', Wi_list[i], u1ss[:, :, s:e])
            chunks.append(h)
        w_heads = jnp.concatenate(chunks, axis=2)
        q, k, v = jnp.split(w_heads, 3, axis=1)
        q = q[:, :, -qlen:]
        klen = k.shape[2]
        q = q.reshape(bsz, N_HEAD, D_HEAD, qlen)
        k = k.reshape(bsz, N_HEAD, D_HEAD, klen)
        v = v.reshape(bsz, N_HEAD, D_HEAD, klen)
        rq = q + r_w_bias[None, :, :, None]
        score = jnp.einsum('bndi,bndj->bnij', rq, k) * SCALE
        prob = jax.nn.softmax(score, axis=-1)
        attn_vec = jnp.einsum('bnij,bndj->bndi', prob, v)
        attn_vec = attn_vec.reshape(bsz, N_HEAD * D_HEAD, qlen)
        attn_out = jnp.einsum('od,bdl->bol', Wo, attn_vec) + bo[None, :, None]
        x = attn_out + z1ss
        m = jnp.mean(x, axis=1, keepdims=True)
        var = jnp.var(x, axis=1, keepdims=True)
        return (x - m) * jax.lax.rsqrt(var + LN_EPS)

    def _L1_xattn_ref(hidden_state, encoder_hidden_state, encoder_attention_mask, Wq, bq, Wk, bk, Wv, bv, Wo, bo, gamma, beta):
        import jax, jax.numpy as jnp
        import numpy as np
        H = 256
        NH = 32
        KVH = 8
        HD = H // NH
        GROUPS = NH // KVH
        EPS = 1e-06
        B, L, S = (4, 128, 128)

        def _gqa_forward(hidden_state, encoder_hidden_state, encoder_attention_mask, Wq, bq, Wk, bk, Wv, bv, Wo, bo, gamma, beta):
            b, l, _ = hidden_state.shape
            s = encoder_hidden_state.shape[1]
            q = hidden_state @ Wq + bq
            k = encoder_hidden_state @ Wk + bk
            v = encoder_hidden_state @ Wv + bv
            q = q.reshape(b, l, KVH, GROUPS, HD).transpose(0, 2, 3, 1, 4)
            k = k.reshape(b, s, KVH, HD).transpose(0, 2, 1, 3)
            v = v.reshape(b, s, KVH, HD).transpose(0, 2, 1, 3)
            scale = 1.0 / jnp.sqrt(jnp.asarray(HD, q.dtype))
            scores = jnp.einsum('bkgld,bksd->bkgls', q, k) * scale
            scores = scores + encoder_attention_mask[:, :, None, :, :]
            attn = jax.nn.softmax(scores, axis=-1)
            out = jnp.einsum('bkgls,bksd->bkgld', attn, v)
            out = out.transpose(0, 3, 1, 2, 4).reshape(b, l, H)
            out = out @ Wo + bo
            x = out + hidden_state
            mu = jnp.mean(x, axis=-1, keepdims=True)
            var = jnp.var(x, axis=-1, keepdims=True)
            return (x - mu) * jax.lax.rsqrt(var + EPS) * gamma + beta
        return _gqa_forward(hidden_state, encoder_hidden_state, encoder_attention_mask, Wq, bq, Wk, bk, Wv, bv, Wo, bo, gamma, beta)

    def _L2_xattn_ref(x, xf_1, xf_2, ln1_scale, ln1_offset, wq1, bq1, wk1, bk1, wv1, bv1, wo1, bo1, bias_k1, bias_v1, ln2_scale, ln2_offset, wq2, bq2, wk2, bk2, wv2, bv2, wo2, bo2, bias_k2, bias_v2, ln_mlp_scale, ln_mlp_offset, w_fc1, b_fc1, w_fc2, b_fc2):
        import jax, jax.numpy as jnp
        import numpy as np
        B, Q, S1, S2 = (4, 32, 256, 256)
        D, H, K, F = (256, 16, 128, 1024)
        LN_EPS = 1e-05

        def _layer_norm(x, scale, offset):
            mu = jnp.mean(x, axis=-1, keepdims=True)
            var = jnp.var(x, axis=-1, keepdims=True)
            return (x - mu) * jax.lax.rsqrt(var + LN_EPS) * scale + offset

        def _cross_attention(q_in, kv_in, wq, bq, wk, bk, wv, bv, wo, bo, bias_k, bias_v):
            b, q_len, _ = q_in.shape
            t = kv_in.shape[1]
            qh = (q_in @ wq + bq).reshape(b, q_len, H, K)
            kh = (kv_in @ wk + bk).reshape(b, t, H, K)
            vh = (kv_in @ wv + bv).reshape(b, t, H, K)
            kh = jnp.concatenate([kh, jnp.broadcast_to(bias_k, (b, 1, H, K))], axis=1)
            vh = jnp.concatenate([vh, jnp.broadcast_to(bias_v, (b, 1, H, K))], axis=1)
            scale = jnp.sqrt(jnp.asarray(K, q_in.dtype))
            logits = jnp.einsum('bqhk,bthk->bhqt', qh, kh) / scale
            weights = jax.nn.softmax(logits, axis=-1)
            ctx = jnp.einsum('bhqt,bthk->bqhk', weights, vh).reshape(b, q_len, H * K)
            return ctx @ wo + bo

        def _forward(x, xf_1, xf_2, ln1_scale, ln1_offset, wq1, bq1, wk1, bk1, wv1, bv1, wo1, bo1, bias_k1, bias_v1, ln2_scale, ln2_offset, wq2, bq2, wk2, bk2, wv2, bv2, wo2, bo2, bias_k2, bias_v2, ln_mlp_scale, ln_mlp_offset, w_fc1, b_fc1, w_fc2, b_fc2):
            res = x
            h = _layer_norm(x, ln1_scale, ln1_offset)
            x = res + _cross_attention(h, xf_1, wq1, bq1, wk1, bk1, wv1, bv1, wo1, bo1, bias_k1, bias_v1)
            res = x
            h = _layer_norm(x, ln2_scale, ln2_offset)
            x = res + _cross_attention(h, xf_2, wq2, bq2, wk2, bk2, wv2, bv2, wo2, bo2, bias_k2, bias_v2)
            h = _layer_norm(x, ln_mlp_scale, ln_mlp_offset)
            h = jax.nn.gelu(h @ w_fc1 + b_fc1, approximate=False) @ w_fc2 + b_fc2
            return x + h
        return _forward(x, xf_1, xf_2, ln1_scale, ln1_offset, wq1, bq1, wk1, bk1, wv1, bv1, wo1, bo1, bias_k1, bias_v1, ln2_scale, ln2_offset, wq2, bq2, wk2, bk2, wv2, bv2, wo2, bo2, bias_k2, bias_v2, ln_mlp_scale, ln_mlp_offset, w_fc1, b_fc1, w_fc2, b_fc2)

    def _L3_xattn_ref(hidden_states, encoder_states, ltor_mask, cross_mask, ln1_s, ln1_b, w_qkv, b_qkv, w_ao, b_ao, ln2_s, ln2_b, w_q, b_q, w_kv, b_kv, w_co, b_co, ln3_s, ln3_b, w1, b1, w2, b2):
        import jax, jax.numpy as jnp
        import numpy as np
        H = 256
        NH = 16
        HD = H // NH
        EPS = 1e-05

        def gelu(x):
            return 0.5 * x * (1.0 + jnp.tanh(0.7978845608028654 * x * (1.0 + 0.044715 * x * x)))

        def layernorm(x, scale, bias):
            m = jnp.mean(x, axis=-1, keepdims=True)
            v = jnp.mean(jnp.square(x - m), axis=-1, keepdims=True)
            return (x - m) * jax.lax.rsqrt(v + EPS) * scale + bias

        def split_heads(x):
            b, s, _ = x.shape
            return x.reshape(b, s, NH, HD).transpose(0, 2, 1, 3)

        def merge_heads(x):
            b, nh, s, hd = x.shape
            return x.transpose(0, 2, 1, 3).reshape(b, s, nh * hd)

        def attention(q, k, v, mask):
            scores = jnp.einsum('bhqd,bhkd->bhqk', q, k) / jnp.sqrt(jnp.float32(HD))
            scores = scores * mask - 10000.0 * (1.0 - mask)
            probs = jax.nn.softmax(scores, axis=-1)
            return jnp.einsum('bhqk,bhkd->bhqd', probs, v)
        ln_out = layernorm(hidden_states, ln1_s, ln1_b)
        qkv = ln_out @ w_qkv + b_qkv
        q, k, v = jnp.split(qkv, 3, axis=-1)
        ctx = merge_heads(attention(split_heads(q), split_heads(k), split_heads(v), ltor_mask))
        attn_out = ctx @ w_ao + b_ao
        x = hidden_states + attn_out
        ln_out = layernorm(x, ln2_s, ln2_b)
        q = ln_out @ w_q + b_q
        kv = encoder_states @ w_kv + b_kv
        k, v = jnp.split(kv, 2, axis=-1)
        ctx = merge_heads(attention(split_heads(q), split_heads(k), split_heads(v), cross_mask))
        cross_out = ctx @ w_co + b_co
        x = x + cross_out
        ln_out = layernorm(x, ln3_s, ln3_b)
        mlp_out = gelu(ln_out @ w1 + b1) @ w2 + b2
        return x + mlp_out
    x = _L0_xattn_ref(x, ctx_2048, L0_xattn_Wqkv0, L0_xattn_Wqkv1, L0_xattn_Winj0, L0_xattn_Winj1, L0_xattn_Wo, L0_xattn_bo, L0_xattn_r_w_bias)
    x = _L1_xattn_ref(x, ctx_2048, mask_Bx1xSxS2_ff0, L1_xattn_Wq, L1_xattn_bq, L1_xattn_Wk, L1_xattn_bk, L1_xattn_Wv, L1_xattn_bv, L1_xattn_Wo, L1_xattn_bo, L1_xattn_gamma, L1_xattn_beta)
    x = _L2_xattn_ref(x, ctx_2048, ctx_2048, L2_xattn_ln1_scale, L2_xattn_ln1_offset, L2_xattn_wq1, L2_xattn_bq1, L2_xattn_wk1, L2_xattn_bk1, L2_xattn_wv1, L2_xattn_bv1, L2_xattn_wo1, L2_xattn_bo1, L2_xattn_bias_k1, L2_xattn_bias_v1, L2_xattn_ln2_scale, L2_xattn_ln2_offset, L2_xattn_wq2, L2_xattn_bq2, L2_xattn_wk2, L2_xattn_bk2, L2_xattn_wv2, L2_xattn_bv2, L2_xattn_wo2, L2_xattn_bo2, L2_xattn_bias_k2, L2_xattn_bias_v2, L2_xattn_ln_mlp_scale, L2_xattn_ln_mlp_offset, L2_xattn_w_fc1, L2_xattn_b_fc1, L2_xattn_w_fc2, L2_xattn_b_fc2)
    x = _L3_xattn_ref(x, ctx_2048, mask_1x1xSxS2_fc1, mask_Bx1xSxS2_ff1, L3_xattn_ln1_s, L3_xattn_ln1_b, L3_xattn_w_qkv, L3_xattn_b_qkv, L3_xattn_w_ao, L3_xattn_b_ao, L3_xattn_ln2_s, L3_xattn_ln2_b, L3_xattn_w_q, L3_xattn_b_q, L3_xattn_w_kv, L3_xattn_b_kv, L3_xattn_w_co, L3_xattn_b_co, L3_xattn_ln3_s, L3_xattn_ln3_b, L3_xattn_w1, L3_xattn_b1, L3_xattn_w2, L3_xattn_b2)
    return x

_drawn_inputs = setup_inputs


def setup_inputs(seed=0):
    import zlib

    import numpy as np

    out = dict(_drawn_inputs(seed))
    spreads = {'L1_xattn_bq': (0.0, 0.8),
     'L1_xattn_bk': (0.0, 2.0),
     'L1_xattn_bv': (0.0, 0.1),
     'L1_xattn_bo': (0.0, 0.1),
     'L1_xattn_gamma': (1.0, 0.2),
     'L1_xattn_beta': (0.0, 0.1),
     'L2_xattn_ln1_scale': (1.0, 0.6),
     'L2_xattn_ln1_offset': (0.0, 0.8),
     'L2_xattn_bq1': (0.0, 0.8),
     'L2_xattn_bk1': (0.0, 2.0),
     'L2_xattn_bv1': (0.0, 0.1),
     'L2_xattn_bo1': (0.0, 0.1),
     'L2_xattn_ln2_scale': (1.0, 0.6),
     'L2_xattn_ln2_offset': (0.0, 0.8),
     'L2_xattn_bq2': (0.0, 0.8),
     'L2_xattn_bk2': (0.0, 2.0),
     'L2_xattn_bv2': (0.0, 0.1),
     'L2_xattn_bo2': (0.0, 0.1),
     'L2_xattn_ln_mlp_scale': (1.0, 0.6),
     'L2_xattn_ln_mlp_offset': (0.0, 0.8),
     'L2_xattn_b_fc1': (0.0, 0.1),
     'L2_xattn_b_fc2': (0.0, 0.1),
     'L3_xattn_ln1_s': (1.0, 0.6),
     'L3_xattn_ln1_b': (0.0, 0.794),
     'L3_xattn_b_qkv': (0.0, 0.28),
     'L3_xattn_b_ao': (0.0, 0.1),
     'L3_xattn_ln2_s': (1.0, 0.6),
     'L3_xattn_ln2_b': (0.0, 2.0),
     'L3_xattn_b_q': (0.0, 2.0),
     'L3_xattn_b_kv': (0.0, 0.286),
     'L3_xattn_b_co': (0.0, 0.1),
     'L3_xattn_ln3_s': (1.0, 0.6),
     'L3_xattn_ln3_b': (0.0, 0.741),
     'L3_xattn_b1': (0.0, 0.1),
     'L3_xattn_b2': (0.0, 0.1)}
    factors = {'L0_xattn_Wqkv0': 8.0,
     'L0_xattn_Wqkv1': 8.0,
     'L0_xattn_Winj0': 8.0,
     'L0_xattn_Winj1': 8.0,
     'L0_xattn_Wo': 8.0,
     'L0_xattn_bo': 64.0,
     'L0_xattn_r_w_bias': 8.0,
     'L1_xattn_Wq': 8.0,
     'L1_xattn_Wk': 8.0,
     'L2_xattn_wq1': 8.0,
     'L2_xattn_wk1': 8.0,
     'L2_xattn_bias_k1': 64.0,
     'L2_xattn_bias_v1': 64.0,
     'L2_xattn_wq2': 8.0,
     'L2_xattn_wk2': 8.0,
     'L2_xattn_bias_k2': 64.0,
     'L2_xattn_bias_v2': 64.0,
     'L3_xattn_w_q': 8.0}
    for name, (base, spread) in spreads.items():
        noise = np.random.default_rng([zlib.crc32(name.encode()), seed]).standard_normal(out[name].shape)
        drawn = base * np.exp(spread * noise) if base else spread * noise
        out[name] = jnp.asarray(drawn.astype(out[name].dtype))
    for name, factor in factors.items():
        out[name] = (out[name] * factor).astype(out[name].dtype)
    return out
```

```python
from contextlib import ExitStack

import numpy as np

import concourse.bass as bass
from concourse import mybir

F32 = mybir.dt.float32
ALU = mybir.AluOpType
ACT = mybir.ActivationFunctionType
AX = mybir.AxisListType

P = 128
B = 8
D = 256
KC = D // P
T = B * P
NPAIR = 8
HALF = T // 2


ROWS = ["l1_bv", "l1_bo", "l1_gamma", "l1_beta", "l2_bo1", "l2_bo2", "l2_b_fc2",
        "l3_bv", "l3_b_ao", "l3_bv2", "l3_b_co", "l3_b2"]
COLS = {}
NCOLS = 0
for _name, _n in [("l0_bo", 1), ("l1_bq", 2), ("l1_bk", 2),
                  ("l2_ln1_scale", 2), ("l2_ln1_offset", 2), ("l2_ln2_scale", 2), ("l2_ln2_offset", 2),
                  ("l2_ln_mlp_scale", 2), ("l2_ln_mlp_offset", 2), ("l2_b_fc1", 8),
                  ("l3_ln1_s", 2), ("l3_ln1_b", 2), ("l3_bq", 2), ("l3_bk", 2),
                  ("l3_ln2_s", 2), ("l3_ln2_b", 2), ("l3_bq2", 2), ("l3_bk2", 2),
                  ("l3_ln3_s", 2), ("l3_ln3_b", 2), ("l3_b1", 8)]:
    COLS[_name] = (NCOLS, _n)
    NCOLS += _n


class Shared:

    def __init__(self, nc, ctx, ins):
        self.nc, self.ctx, self.ins = nc, ctx, ins
        self.shared = {}

        def sb(name, shape):
            return ctx.enter_context(nc.sbuf_tensor(name, shape, F32))

        self.sb = sb
        self.x = sb("x_residual", [P, B, D])
        self.hT = sb("hT", [P, KC, T])
        self.cT = sb("ctxT", [P, KC, T])
        self.big = sb("big", [P, 8192])
        self.qT = sb("qT", [P, 2 * T])
        self.kT = sb("kT", [P, 2 * B * (P + 1)])
        self.v = sb("v", [P, B, D])
        self.E = sb("probs", [P, 4, 1024])
        self.PT = sb("probsT", [P, 2, 1024])
        self.sm = sb("masked_scores", [P, 4, 512])
        self.km = sb("masked_keys", [P, 3, 512])
        self.cx = sb("ctx_small", [P, 2, D])
        self.hn = sb("normalised", [P, 4, D])
        self.wA = sb("weights_a", [P, 2048])
        self.wB = sb("weights_b", [P, 2 * D + 2])
        self.w1 = sb("w_fc1", [P, KC, 1024])
        self.w2 = sb("w_fc2", [P, 8, D])
        self.wC = sb("weights_c", [P, 2048])
        self.rows = sb("bias_rows", [P, len(ROWS), D])
        self.bv = sb("value_bias_rows", [P, 2, D])
        self.mask = sb("mask", [P, B, P])
        self.amask = sb("additive_mask", [P, B, P])
        self.st = sb("stats", [P, 256])
        self.cols = sb("bias_cols", [P, NCOLS])
        self.eps = sb("eps", [P, 2])
        self.consts = sb("consts", [P, 128 + 128 + 16 + 8])
        self.ident = self.consts[:, 0:128]
        self.mean_mat = self.consts[:, 128:256]
        self.head8 = self.consts[:, 256:272]
        self.head16 = self.consts[:, 272:280]
        self.acc = [ctx.enter_context(nc.psum_tensor(f"acc{i}", [P, 512], F32)) for i in range(4)]
        self.pS = [ctx.enter_context(nc.psum_tensor(f"pS{i}", [P, 512], F32)) for i in range(2)]
        self.pT = ctx.enter_context(nc.psum_tensor("pT", [P, 512], F32))
        self.pC = ctx.enter_context(nc.psum_tensor("pC", [P, 512], F32))

    def row(self, name):
        return self.rows[:, ROWS.index(name), :]

    def col(self, name):
        at, n = COLS[name]
        return self.cols[:, at:at + n]

    def counts(self, kind, **totals):
        out = []
        for name, total in totals.items():
            if (kind, name) not in self.shared:
                self.shared[kind, name] = [self.sem(f"{kind}_{name}"), 0]
            entry = self.shared[kind, name]
            out.append(Count(*entry))
            entry[1] += total
        return out

    def sem(self, name):
        return self.ctx.enter_context(self.nc.semaphore(name))


class Count:

    def __init__(self, sem, base):
        self.sem, self.base = sem, base


def wait(e, count, value):
    if isinstance(count, Count):
        e.wait_ge(count.sem, count.base + value)
    else:
        e.wait_ge(count, value)


class Ring:

    def __init__(self, kinds, depth):
        self.kinds, self.depth = kinds, depth

    def before(self, n, i):
        m = n - self.depth
        if m < 0:
            if isinstance(i, int) and i == 0:
                return None
            m, i = m + len(self.kinds), i - 1
        kind = self.kinds[m]
        return kind, i * self.kinds.count(kind) + self.kinds[:m + 1].count(kind)


class Layer0:

    SCALE = 64 ** -0.5
    PACK = 12 * P + 1

    def __init__(self, g):
        self.g = g
        s = g.sem
        self.loaded = s("l0_inputs_loaded")
        self.w_loaded = s("l0_pair_weights_loaded")
        self.wo_loaded = s("l0_wo_loaded")
        self.consts_set = s("l0_key_zeros_set")
        self.s_full = s("l0_s_bank_full")
        self.s_free = s("l0_s_bank_free")
        self.v_full = s("l0_values_in_bank")
        self.v_ready = s("l0_values_ready")
        self.t_full = s("l0_t_bank_full")
        self.pt0 = s("l0_probsT_half0_ready")
        self.pt1 = s("l0_probsT_half1_ready")
        self.c_full = s("l0_c_bank_full")
        self.ctx = s("l0_ctx_ready")
        self.acc_done = s("l0_acc_units_done")
        self.max = s("l0_max_ready")
        self.nmax = s("l0_negmax_ready")
        self.exp = s("l0_exp_ready")
        self.rec = s("l0_recip_ready")
        self.norm0 = s("l0_probs_half0_normalised")
        self.norm1 = s("l0_probs_half1_normalised")
        self.f_x = s("l0_sum_ready")
        self.f_mean = s("l0_mean_ready")
        self.f_xc = s("l0_centered_ready")
        self.f_sq = s("l0_square_ready")
        self.f_var = s("l0_var_ready")
        self.f_sd = s("l0_std_ready")
        self.f_rs = s("l0_rstd_ready")
        self.x_done = s("l0_output_ready")
        self.z = g.big[:, 0:2048].rearrange("p (b l) -> p b l", b=B)
        self.u = g.big[:, 2048:4096].rearrange("p (b l) -> p b l", b=B)
        self.kz = g.big[:, 4096:8192].rearrange("p (b h l) -> p b h l", b=B, h=2)
        self.qT = g.qT[:, :].rearrange("p (b l) -> p b l", b=B)
        self.v = g.v[:, :, :].rearrange("p b (j n) -> p b j n", j=2)
        self.w = g.wA[:, 0:12 * P].rearrange("p (q m o) -> p q m o", q=3, m=4)
        self.rwb = g.wA[:, 12 * P:12 * P + 1]
        self.wo = g.wB[:, 0:P]
        self.E = g.E[:, :, :].rearrange("p n (i h l) -> p n i h l", i=2, h=2)
        self.PT = g.PT[:, :, :].rearrange("p n (j h l) -> p n j h l", j=2, h=2)
        self.st = g.st[:, 0:64].rearrange("p (k n i h) -> p k n i h", k=4, n=4, i=2)
        self.bo = g.col("l0_bo")
        self.eps = g.eps[:, 0:1]

    def sp(self, e):
        g, ins = self.g, self.g.ins
        e.dma_start(self.z, ins["x_dbl"].rearrange("p (b l) -> p b l", b=B)).then_inc(self.loaded, 16)
        e.dma_start(g.wA[:, 0:self.PACK], ins["l0_w"][0]).then_inc(self.w_loaded, 16)
        e.dma_start(self.u, ins["ctx_dbl"].rearrange("p (b l) -> p b l", b=B)).then_inc(self.loaded, 16)
        e.dma_start(g.consts[:, :], ins["consts"]).then_inc(self.loaded, 16)
        e.dma_start(g.cols[:, :], ins["cols"]).then_inc(self.loaded, 16)
        e.dma_start(self.wo, ins["l0_wo"][0]).then_inc(self.wo_loaded, 16)
        e.dma_start(g.cT[:, :, :], ins["ctxT"]).then_inc(self.loaded, 16)
        e.dma_start(g.rows[:, :, :].rearrange("p r n -> p (r n)"),
                    ins["rows"].broadcast_to([P, len(ROWS) * D])).then_inc(self.loaded, 16)

        def pair(p):
            e.wait_ge(self.v_ready, 8 * p)
            e.wait_ge(self.s_free, 24 * p - 16)
            e.dma_start(g.wA[:, 0:self.PACK], self.at(ins["l0_w"], p)).then_inc(self.w_loaded, 16)
            e.wait_ge(self.acc_done, 8 * p)
            e.dma_start(self.wo, self.at(ins["l0_wo"], p)).then_inc(self.wo_loaded, 16)

        with e.Fori(1, NPAIR) as p:
            pair(p)

    @staticmethod
    def at(array, p):
        return array[bass.ds(p, 1)].rearrange("a p n -> (a p) n")

    def pe(self, e):
        g = self.g
        ring = Ring(["act"] * 24, 2)
        bank = g.pS

        def claim(n, p):
            need = ring.before(n, p)
            if need is not None:
                e.wait_ge(self.s_free, need[1])

        def project_qk(p):
            e.wait_ge(self.w_loaded, 16 * (p + 1))
            n = 0
            for q in range(2):
                for chunk in range(2):
                    for half in range(2):
                        claim(n, p)
                        for m, src in enumerate((self.z, self.u)):
                            mm = e.matmul(bank[n % 2][:, :], self.w[:, q, 2 * chunk + m, :],
                                          src[:, 4 * half:4 * half + 4, chunk * P:chunk * P + P],
                                          start=m == 0, stop=m == 1)
                        mm.then_inc(self.s_full, 1)
                        n += 1

        def project_v(b, p):
            if b >= 2:
                e.wait_ge(self.v_ready, 8 * p + b - 1)
            elif not (isinstance(p, int) and p == 0):
                e.wait_ge((self.pt1, self.ctx)[b], 8 * p)
            for j in range(2):
                for m, src in enumerate((self.z, self.u)):
                    mm = e.matmul((g.pT, g.pC)[b % 2][:, j * P:j * P + P], src[:, b, j * P:j * P + P],
                                  self.w[:, 2, 2 * j + m, :], start=m == 0, stop=m == 1)
            mm.then_inc(self.v_full, 1)

        def scores(u, it, p):
            claim(8 + 2 * u + it, p)
            if (u, it) == (0, 0):
                e.wait_ge(self.s_free, 24 * p + 8)
            e.matmul(bank[it][:, :], self.qT[:, u, it * P:it * P + P],
                     self.kz[:, u, :, :], start=True, stop=True).then_inc(self.s_full, 1)

        def transposes(u, jt, p):
            if jt == 0:
                e.wait_ge(self.norm0, 8 * p + u + 1)
                e.wait_ge(self.norm1, 8 * p + u + 1)
                if u == 0:
                    e.wait_ge(self.v_ready, 8 * p + 7)
                if not (isinstance(p, int) and p == 0 and u == 0):
                    e.wait_ge(self.pt1, 8 * p + u)
            else:
                e.wait_ge(self.pt0, 8 * p + u + 1)
            for h in range(2):
                for it in range(2):
                    mm = e.transpose(g.pT[:, (2 * h + it) * P:(2 * h + it + 1) * P],
                                     self.E[:, u % 4, it, h, jt * P:jt * P + P], g.ident)
            mm.then_inc(self.t_full, 1)

        def context(u, h, p):
            if h == 0:
                if u == 0:
                    e.wait_ge(self.v_ready, 8 * p + 8)
                e.wait_ge(self.pt0, 8 * p + u + 1)
                e.wait_ge(self.pt1, 8 * p + u + 1)
                if not (isinstance(p, int) and p == 0 and u == 0):
                    e.wait_ge(self.ctx, 8 * p + u)
            for j in range(2):
                mm = e.matmul(g.pC[64 * h:64 * h + 64, 0:D], self.v[:, u, j, 64 * h:64 * h + 64],
                              self.PT[:, u % 2, j, h, :], start=j == 0, stop=j == 1)
            if h == 1:
                mm.then_inc(self.c_full, 1)

        def output(u, p, first):
            e.wait_ge(self.ctx, 8 * p + u + 1)
            if u == 0:
                e.wait_ge(self.wo_loaded, 16 * (p + 1))
            e.matmul(g.acc[u // 2][:, (u % 2) * D:(u % 2) * D + D], self.wo, g.cx[:, u % 2, :],
                     start=first and u % 2 == 0, stop=True, skip_group_check=True)\
                .then_inc(self.acc_done, 1)

        def steps(slots, p, first):
            for s in slots:
                for it in range(2):
                    if s < B:
                        scores(s, it, p)
                    if s < 2:
                        project_v(4 + 2 * s + it, p)
                    if 0 <= s - 2 < B:
                        transposes(s - 2, it, p)
                    if 0 <= s - 3 < B:
                        context(s - 3, it, p)
                if 0 <= s - 4 < B:
                    output(s - 4, p, first)

        e.wait_ge(self.loaded, 96)
        e.wait_ge(self.consts_set, 4)
        project_qk(0)
        for b in range(4):
            project_v(b, 0)
        steps(range(B), 0, True)

        def pair(p, first):
            steps(range(B, B + 1), p - 1, first)
            project_qk(p)
            steps(range(B + 1, B + 4), p - 1, first)
            for b in range(4):
                project_v(b, p)
            steps(range(B), p, False)

        pair(1, True)
        with e.Fori(2, NPAIR) as p:
            pair(p, False)
        steps(range(B, B + 4), NPAIR - 1, False)
        for c in range(4):
            e.wait_ge(self.f_x, c + 1)
            if c >= 2:
                e.wait_ge(self.f_xc, c - 1)
            e.matmul(g.pS[c % 2][:, :], g.mean_mat, self.xs(c), start=True, stop=True)\
                .then_inc(self.f_mean, 1)
            if c >= 1:
                self.pe_var(e, c - 1)
        self.pe_var(e, 3)

    def pe_var(self, e, c):
        g = self.g
        e.wait_ge(self.f_sq, c + 1)
        if c >= 2:
            e.wait_ge(self.f_sd, c - 1)
        e.matmul((g.pT, g.pC)[c % 2][:, :], g.mean_mat, g.sm[:, c % 2, :], start=True, stop=True)\
            .then_inc(self.f_var, 1)

    def xs(self, c):
        return self.g.x[:, 2 * c:2 * c + 2, :].rearrange("p b l -> p (b l)")

    def act(self, e):
        g = self.g
        bank = g.pS

        def evacuate_qk(p):
            n = 0
            for q in range(2):
                for chunk in range(2):
                    for half in range(2):
                        e.wait_ge(self.s_full, 24 * p + n + 1)
                        src = bank[n % 2][:, :].rearrange("p (b l) -> p b l", b=4)
                        bs, ls = slice(4 * half, 4 * half + 4), slice(chunk * P, chunk * P + P)
                        if q == 0:
                            i = e.activation(self.qT[:, bs, ls], src, ACT.Identity, bias=self.rwb)
                        else:
                            e.activation(self.kz[0:64, bs, 0, ls], src[0:64], ACT.Copy)
                            i = e.activation(self.kz[64:128, bs, 1, ls], src[64:128], ACT.Copy)
                        i.then_inc(self.s_free, 1)
                        n += 1

        def exps(u, it, p):
            e.wait_ge(self.nmax, 16 * p + 2 * u + it + 1)
            e.wait_ge(self.s_full, 24 * p + 8 + 2 * u + it + 1)
            if not isinstance(p, int) or p > 0 or u >= 4:
                e.wait_ge(self.t_full, 16 * p + 2 * (u - 4) + 2)
                e.wait_ge((self.norm0, self.norm1)[it], 8 * p + u - 3)
            for h in range(2):
                i = e.activation(self.E[:, u % 4, it, h, :], bank[it][:, h * D:h * D + D], ACT.Exp,
                                 bias=self.st[:, 1, u % 4, it, h:h + 1], scale=self.SCALE,
                                 accum_out=self.st[:, 2, u % 4, it, h:h + 1])
            i.then_inc(self.s_free, 1)

        def evacuate_t(u, p):
            e.wait_ge(self.t_full, 16 * p + 2 * u + 2)
            e.activation(self.PT[:, u % 2, 1, :, :], g.pT[:, :].rearrange("p (h l) -> p h l", h=2),
                         ACT.Copy).then_inc(self.pt1, 1)

        def steps(slots, p):
            for s in slots:
                if s < B:
                    exps(s, 0, p)
                if 0 <= s - 2 < B:
                    evacuate_t(s - 2, p)
                if s < B:
                    exps(s, 1, p)

        evacuate_qk(0)
        steps(range(B), 0)

        def pair(p):
            steps(range(B, B + 1), p - 1)
            evacuate_qk(p)
            steps(range(B + 1, B + 4), p - 1)
            steps(range(B), p)

        with e.Fori(1, NPAIR) as p:
            pair(p)
        steps(range(B, B + 4), NPAIR - 1)
        for c in range(4):
            e.wait_ge(self.f_xc, c + 1)
            if c >= 2:
                e.wait_ge(self.f_var, c - 1)
            e.activation(g.sm[:, c % 2, :], self.xs(c), ACT.Square).then_inc(self.f_sq, 1)
        for c in range(4):
            e.wait_ge(self.f_var, c + 1)
            e.activation(g.E[:, c, 0:512], (g.pT, g.pC)[c % 2][:, :], ACT.Sqrt, bias=self.eps)\
                .then_inc(self.f_sd, 1)

    def dve(self, e):
        g = self.g
        bank = g.pS

        def maxes(u, it, p):
            e.wait_ge(self.s_full, 24 * p + 8 + 2 * u + it + 1)
            e.tensor_reduce(self.st[:, 0, u % 4, it, :],
                            bank[it][:, :].rearrange("p (h l) -> p h l", h=2), AX.X, ALU.max)\
                .then_inc(self.max, 1)
            e.wait_ge(self.max, 16 * p + 2 * u + it + 1)
            e.tensor_scalar(self.st[:, 1, u % 4, it, :], self.st[:, 0, u % 4, it, :], -self.SCALE,
                            None, ALU.mult).then_inc(self.nmax, 1)

        def reciprocals(u, it, p):
            e.wait_ge(self.s_free, 24 * p + 8 + 2 * u + it + 1)
            e.reciprocal(self.st[:, 3, u % 4, it, :], self.st[:, 2, u % 4, it, :])\
                .then_inc(self.rec, 1)

        def normalise(u, p):
            e.wait_ge(self.rec, 16 * p + 2 * u + 2)
            for h in range(2):
                i = e.tensor_scalar(self.E[:, u % 4, 1, h, :], self.E[:, u % 4, 1, h, :],
                                    self.st[:, 3, u % 4, 1, h:h + 1], None, ALU.mult)
            i.then_inc(self.norm1, 1)

        def evacuate_t(u, p):
            e.wait_ge(self.t_full, 16 * p + 2 * u + 1)
            e.tensor_copy(self.PT[:, u % 2, 0, :, :], g.pT[:, :].rearrange("p (h l) -> p h l", h=2))\
                .then_inc(self.pt0, 1)

        def evacuate_c(u, p):
            e.wait_ge(self.c_full, 8 * p + u + 1)
            if not (isinstance(p, int) and p == 0 and u < 2):
                e.wait_ge(self.acc_done, 8 * p + u - 1)
            e.tensor_copy(g.cx[:, u % 2, :], g.pC[:, 0:D]).then_inc(self.ctx, 1)

        def evacuate_v(b, p):
            e.wait_ge(self.v_full, 8 * p + b + 1)
            e.tensor_copy(g.v[:, b, :], (g.pT, g.pC)[b % 2][:, 0:D]).then_inc(self.v_ready, 1)

        def steps(slots, p):
            for s in slots:
                if 0 <= s - 2 < B:
                    evacuate_t(s - 2, p)
                if 0 <= s - 1 < B:
                    reciprocals(s - 1, 1, p)
                    normalise(s - 1, p)
                if s < B:
                    maxes(s, 0, p)
                if s < 2:
                    evacuate_v(4 + 2 * s, p)
                if s < B:
                    reciprocals(s, 0, p)
                    maxes(s, 1, p)
                if s < 2:
                    evacuate_v(5 + 2 * s, p)
                if 0 <= s - 3 < B:
                    evacuate_c(s - 3, p)

        def pair(p):
            for b in range(4):
                evacuate_v(b, p)
            steps(range(B), p)

        pair(0)
        with e.Fori(1, NPAIR) as p:
            steps(range(B, B + 4), p - 1)
            pair(p)
        steps(range(B, B + 4), NPAIR - 1)
        for c in range(4):
            e.wait_ge(self.acc_done, 8 * (NPAIR - 1) + 2 * c + 2)
            e.scalar_tensor_tensor(out=self.xs(c), in0=g.acc[c][:, :], scalar=self.bo,
                                   in1=self.z[:, 2 * c:2 * c + 2, :].rearrange("p b l -> p (b l)"),
                                   op0=ALU.add, op1=ALU.add).then_inc(self.f_x, 1)
        for c in range(4):
            e.wait_ge(self.f_mean, c + 1)
            e.tensor_tensor(self.xs(c), self.xs(c), g.pS[c % 2][:, :], ALU.subtract)\
                .then_inc(self.f_xc, 1)
        for c in range(4):
            e.wait_ge(self.f_sd, c + 1)
            e.reciprocal(g.PT[:, c % 2, 0:512], g.E[:, c, 0:512]).then_inc(self.f_rs, 1)
            e.wait_ge(self.f_rs, c + 1)
            e.wait_ge(self.f_sq, c + 1)
            e.tensor_tensor(self.xs(c), self.xs(c), g.PT[:, c % 2, 0:512], ALU.mult)\
                .then_inc(self.x_done, 2)
            if c >= 1:
                e.wait_ge(self.x_done, 2 * c)

    def pool(self, e):
        g = self.g
        e.memset(self.kz[64:128, :, 0, :], 0.0).then_inc(self.consts_set, 1)
        e.wait_ge(self.consts_set, 1)
        e.memset(self.kz[0:64, :, 1, :], 0.0).then_inc(self.consts_set, 1)
        e.wait_ge(self.consts_set, 2)
        e.memset(self.eps, 1e-5).then_inc(self.consts_set, 1)
        e.wait_ge(self.consts_set, 3)
        e.memset(g.eps[:, 1:2], -0.5).then_inc(self.consts_set, 1)

        def pair(p):
            for u in range(B):
                e.wait_ge(self.rec, 16 * p + 2 * u + 1)
                e.tensor_tensor(self.E[:, u % 4, 0, :, :], self.E[:, u % 4, 0, :, :],
                                self.st[:, 3, u % 4, 0, :].unsqueeze(2).broadcast_to([P, 2, D]),
                                ALU.mult).then_inc(self.norm0, 1)

        pair(0)
        with e.Fori(1, NPAIR) as p:
            pair(p)


class NormT:

    def __init__(self, g, name, dst, x_ready, prev, norm=None):
        self.g, self.dst, self.x_ready, self.prev, self.norm = g, dst, x_ready, prev, norm
        (self.stats, self.aggr, self.veps, self.rstd, self.h, self.t_full, self.done) = g.counts(
            "norm_t" if norm else "plain_t", stats_ready=B, mean_var_ready=B, var_eps_ready=B, rstd_ready=B,
            normalised_ready=B, transposed_in_bank=B, transposed_ready=B)
        self.bn = g.st[:, 64:112].rearrange("p (b k) -> p b k", b=B)
        self.mv = g.st[:, 112:128].rearrange("p (b k) -> p b k", b=B)
        self.ve = g.st[:, 128:136]
        self.rs = g.st[:, 136:144]
        self.banks = [g.pT, g.pC]

    def sp(self, e):
        pass

    def dve(self, e):
        g = self.g
        if not self.norm:
            return
        for b in range(B + 1):
            if b < B:
                wait(e, self.x_ready[0], self.x_ready[1](b))
                e.bn_stats(self.bn[:, b, :], g.x[:, b, :]).then_inc(self.stats.sem, 1)
                wait(e, self.stats, b + 1)
                e.bn_aggr(self.mv[:, b, :], self.bn[:, b, :]).then_inc(self.aggr.sem, 1)
            if b >= 1:
                c = b - 1
                wait(e, self.rstd, c + 1)
                if c >= 4:
                    wait(e, self.t_full, c - 3)
                e.tensor_scalar(g.hn[:, c % 4, :], g.x[:, c, :], self.mv[:, c, 0:1],
                                self.rs[:, c:c + 1], ALU.subtract, ALU.mult).then_inc(self.h.sem, 1)

    def pool(self, e):
        g = self.g
        if not self.norm:
            return
        for b in range(B):
            wait(e, self.aggr, b + 1)
            e.tensor_scalar(self.ve[:, b:b + 1], self.mv[:, b, 1:2], 1e-5, None, ALU.add)\
                .then_inc(self.veps.sem, 1)
            wait(e, self.veps, b + 1)
            e.tensor_tensor(self.rs[:, b:b + 1], self.ve[:, b:b + 1], g.eps[:, 1:2], ALU.pow)\
                .then_inc(self.rstd.sem, 1)
            wait(e, self.rstd, b + 1)

    def pe(self, e):
        g = self.g
        for sem, value in self.prev:
            wait(e, sem, value)
        for b in range(B):
            if self.norm:
                wait(e, self.h, b + 1)
            else:
                wait(e, self.x_ready[0], self.x_ready[1](b))
            if b >= 2:
                wait(e, self.done, b - 1)
            for c in range(KC):
                src = g.hn[:, b % 4, c * P:c * P + P] if self.norm else g.x[:, b, c * P:c * P + P]
                mm = e.transpose(self.banks[b % 2][:, c * P:c * P + P], src, g.ident)
            mm.then_inc(self.t_full.sem, 1)

    def act(self, e):
        for b in range(B):
            wait(e, self.t_full, b + 1)
            bank = self.banks[b % 2]
            if self.norm:
                scale, offset = self.norm
                for c in range(KC):
                    i = e.activation(self.dst[:, c, b * P:b * P + P], bank[:, c * P:c * P + P],
                                     ACT.Identity, scale=scale[:, c:c + 1], bias=offset[:, c:c + 1])
            else:
                i = e.activation(self.dst[:, :, b * P:b * P + P],
                                 bank[:, 0:D].rearrange("p (c t) -> p c t", c=KC), ACT.Copy)
            i.then_inc(self.done.sem, 1)

    def read_x(self):
        return (self.h, B) if self.norm else (self.t_full, B)

    def drained(self):
        return [(self.done, B)]


class Project:

    def __init__(self, g, name, prev, w_loaded, q_src, kv_src, wq, wk, wv, bq, bk, bv, groups):
        self.g, self.prev, self.w_loaded = g, prev, w_loaded
        self.srcs, self.ws, self.bs = (q_src, kv_src), (wq, wk), (bq, bk)
        self.kv_src, self.wv, self.bv, self.groups = kv_src, wv, bv, groups
        (self.full, self.qk, self.vs, self.ones) = g.counts(
            "project", projection_in_bank=16, q_k_ready=8, v_ready=B, v_ones_set=2)
        self.qT = g.qT[:, :].rearrange("p (m t) -> p m t", m=2)
        self.kT = g.kT[:, 0:2 * T].rearrange("p (m t) -> p m t", m=2)
        self.vx = g.big[:, 4096:8192].rearrange("p (b g n) -> p b g n", b=B, g=4)
        self.banks = g.acc

    def sp(self, e):
        pass

    def pe(self, e):
        for sem, value in self.prev + self.w_loaded:
            wait(e, sem, value)
        n = 0
        for which in range(2):
            for m in range(2):
                for half in range(2):
                    if n >= 4:
                        wait(e, self.qk, n - 3)
                    for c in range(KC):
                        mm = e.matmul(self.banks[n % 4][:, :],
                                      self.ws[which][:, c, m * P:m * P + P],
                                      self.srcs[which][:, c, half * HALF:half * HALF + HALF],
                                      start=c == 0, stop=c == KC - 1)
                    mm.then_inc(self.full.sem, 1)
                    n += 1
        width = self.wv.shape[2]
        for b in range(B):
            if b < 4:
                wait(e, self.qk, 5 + b)
            else:
                wait(e, self.vs, b - 3)
            for c in range(KC):
                mm = e.matmul(self.banks[b % 4][:, 0:width], self.kv_src[:, c, b * P:b * P + P],
                              self.wv[:, c, :], start=c == 0, stop=c == KC - 1)
            mm.then_inc(self.full.sem, 1)

    def act(self, e):
        n = 0
        for which, dst in enumerate((self.qT, self.kT)):
            for m in range(2):
                for half in range(2):
                    wait(e, self.full, n + 1)
                    e.activation(dst[:, m, half * HALF:half * HALF + HALF], self.banks[n % 4][:, :],
                                 ACT.Identity, bias=self.bs[which][:, m:m + 1]).then_inc(self.qk.sem, 1)
                    n += 1

    def dve(self, e):
        n = 64 * self.groups
        wait(e, self.ones, 2)
        for b in range(B):
            wait(e, self.full, 8 + b + 1)
            e.tensor_tensor(self.vx[:, b, 0:self.groups, 0:64],
                            self.banks[b % 4][:, 0:n].rearrange("p (g n) -> p g n", g=self.groups),
                            self.bv[:, 0:n].rearrange("p (g n) -> p g n", g=self.groups),
                            ALU.add).then_inc(self.vs.sem, 1)

    def pool(self, e):
        for sem, value in self.prev:
            wait(e, sem, value)
        e.memset(self.vx[:, :, 0:self.groups, 64:65], 1.0).then_inc(self.ones.sem, 1)
        wait(e, self.ones, 1)
        e.memset(self.vx[:, :, 0:self.groups, 65:128], 0.0).then_inc(self.ones.sem, 1)

    def drained(self):
        return [(self.qk, 8), (self.vs, B), (self.ones, 2)]


class SmallHeads:

    def __init__(self, g, name, prev, hd, scale, multiply, masks_ready):
        self.g, self.prev, self.hd, self.scale, self.multiply = g, prev, hd, scale, multiply
        self.masks_ready = masks_ready
        self.one_mask = False
        self.G = (8 if hd == 8 else 4)
        self.per_tile = self.G // 2
        self.heads = g.head8 if hd == 8 else g.head16
        self.N = B * self.G
        (self.keys, self.s_full, self.scaled, self.masked, self.min, self.exp,
         self.t_full, self.pt, self.c_full, self.rec, self.done) = g.counts(
            "small_heads", keys_masked=self.N, scores_in_bank=self.N,
            scores_scaled=self.N, scores_masked=self.N if multiply else 0, min_ready=self.N,
            exp_ready=self.N, transposed_in_bank=self.N, probsT_ready=self.N,
            context_in_bank=self.N, recip_ready=self.N, context_ready=self.N)
        if not multiply:
            self.masked = self.scaled
        self.qT = g.qT[:, :].rearrange("p (m t) -> p m t", m=2)
        self.kT = g.kT[:, 0:2 * T].rearrange("p (m t) -> p m t", m=2)
        self.vx = g.big[:, 4096:8192].rearrange("p (b g n) -> p b g n", b=B, g=4)
        self.km = g.km[:, :, :].rearrange("p n (j t) -> p n j t", j=4)
        self.sm = g.sm[:, :, :].rearrange("p n (j t) -> p n j t", j=4)
        self.E = g.E[:, :, 0:512].rearrange("p n (j t) -> p n j t", j=4)
        self.PT = g.PT[:, :, 0:512].rearrange("p n (j t) -> p n j t", j=4)
        self.mn = g.st[:, 160:176].rearrange("p (n j) -> p n j", n=4)
        self.rc = g.st[:, 176:192].rearrange("p (n j) -> p n j", n=4)
        self.bS = g.pS
        self.bT = [g.pT, g.acc[0]]
        self.bC = [g.pC, g.acc[1]]

    def sp(self, e):
        pass

    def unit(self, n):
        b, gr = divmod(n, self.G)
        return b, gr, gr // self.per_tile, 4 * (gr % self.per_tile)

    def pool(self, e):
        for sem, value in self.prev + self.masks_ready:
            wait(e, sem, value)
        for n in range(self.N + 1):
            if n < self.N:
                b, _, m, h = self.unit(n)
                if n >= 3:
                    wait(e, self.s_full, n - 2)
                e.tensor_tensor(self.km[:, n % 3], self.kT[:, m, b * P:b * P + P].unsqueeze(1)
                                .broadcast_to([P, 4, P]),
                                self.heads[:, h:h + 4].unsqueeze(2).broadcast_to([P, 4, P]),
                                ALU.mult).then_inc(self.keys.sem, 1)
            if self.multiply and n >= 1:
                k = n - 1
                b = self.unit(k)[0]
                wait(e, self.scaled, k + 1)
                e.tensor_tensor(self.sm[:, k % 4], self.sm[:, k % 4], self.amask(b), ALU.subtract)\
                    .then_inc(self.masked.sem, 1)

    def mul_mask(self, b):
        b = 0 if self.one_mask else b
        return self.g.mask[:, b, :].unsqueeze(1).broadcast_to([P, 4, P])

    def amask(self, b):
        b = 0 if self.one_mask else b
        return self.g.amask[:, b, :].unsqueeze(1).broadcast_to([P, 4, P])

    def pe(self, e):
        g = self.g
        for sem, value in self.prev:
            wait(e, sem, value)
        for s in range(self.N + 4):
            if s < self.N:
                n = s
                b, _, m, _ = self.unit(n)
                wait(e, self.keys, n + 1)
                if n >= 2:
                    wait(e, self.scaled, n - 1)
                e.matmul(self.bS[n % 2][:, :], self.qT[:, m, b * P:b * P + P], self.km[:, n % 3],
                         start=True, stop=True).then_inc(self.s_full.sem, 1)
            n = s - 3
            if 0 <= n < self.N:
                wait(e, self.exp, n + 1)
                if n >= 2:
                    wait(e, self.pt, n - 1)
                for j in range(4):
                    mm = e.transpose(self.bT[n % 2][:, j * P:j * P + P], self.E[:, n % 4, j, :],
                                     g.ident)
                mm.then_inc(self.t_full.sem, 1)
            n = s - 4
            if 0 <= n < self.N:
                b, gr, _, _ = self.unit(n)
                wait(e, self.pt, n + 1)
                if n >= 2:
                    wait(e, self.done, n - 1)
                for j in range(4):
                    mm = e.matmul(self.bC[n % 2][:, j * P:j * P + P], self.PT[:, n % 2, j, :],
                                  self.vx[:, b, 0 if self.hd == 8 else gr, :], start=True, stop=True)
                mm.then_inc(self.c_full.sem, 1)

    def act(self, e):
        for s in range(self.N + 2):
            n = s - 2
            if n >= 0:
                wait(e, self.t_full, n + 1)
                e.activation(self.PT[:, n % 2], self.bT[n % 2][:, :]
                             .rearrange("p (j t) -> p j t", j=4), ACT.Copy).then_inc(self.pt.sem, 1)
            n = s
            if n < self.N:
                wait(e, self.min, n + 1)
                if n >= 4:
                    wait(e, self.t_full, n - 3)
                for j in range(4):
                    i = e.activation(self.E[:, n % 4, j, :], self.sm[:, n % 4, j, :], ACT.Exp,
                                     bias=self.mn[:, n % 4, j:j + 1], scale=-1.0)
                i.then_inc(self.exp.sem, 1)

    def dve(self, e):
        g, hd = self.g, self.hd
        for sem, value in self.masks_ready:
            wait(e, sem, value)
        for s in range(self.N + 5):
            n = s
            if n < self.N:
                b = self.unit(n)[0]
                wait(e, self.s_full, n + 1)
                if n >= 4:
                    wait(e, self.exp, n - 3)
                e.scalar_tensor_tensor(out=self.sm[:, n % 4],
                                       in0=self.bS[n % 2][:, :].rearrange("p (j t) -> p j t", j=4),
                                       scalar=-self.scale, in1=self.mul_mask(b), op0=ALU.mult,
                                       op1=ALU.mult if self.multiply else ALU.subtract)\
                    .then_inc(self.scaled.sem, 1)
            n = s - 1
            if 0 <= n < self.N:
                wait(e, self.masked, n + 1)
                e.tensor_reduce(self.mn[:, n % 4, :], self.sm[:, n % 4], AX.X, ALU.min)\
                    .then_inc(self.min.sem, 1)
            n = s - 5
            if n >= 0:
                b, gr, _, _ = self.unit(n)
                bank = self.bC[n % 2]
                wait(e, self.c_full, n + 1)
                e.reciprocal(self.rc[:, n % 4, :],
                             bank[:, :].rearrange("p (j c) -> p j c", j=4)[:, :, 64])\
                    .then_inc(self.rec.sem, 1)
                wait(e, self.rec, n + 1)
                step, first = (P, hd * gr) if hd == 8 else (P + hd, 0)
                src = bass.AP(tensor=bank, offset=first, ap=[[512, P], [step, 4], [1, hd]])
                e.tensor_tensor(g.v[:, b, 4 * hd * gr:4 * hd * (gr + 1)]
                                .rearrange("p (j d) -> p j d", j=4), src,
                                self.rc[:, n % 4, :].unsqueeze(2).broadcast_to([P, 4, hd]),
                                ALU.mult).then_inc(self.done.sem, 1)

    def drained(self):
        return [(self.done, self.N), (self.pt, self.N)]


class OutProject:

    def __init__(self, g, name, prev, heads, wo, bo, x_read, w_loaded):
        self.g, self.prev, self.heads, self.wo, self.bo = g, prev, heads, wo, bo
        self.x_read, self.w_loaded = x_read, w_loaded
        (self.xb, self.t_full, self.cx, self.o_full, self.x) = g.counts(
            "out_project", x_plus_bias_ready=B, transposed_in_bank=B, contextT_ready=B,
            output_in_bank=B, x_ready=B)
        self.bT = [g.acc[2], g.acc[3]]
        self.bO = [g.pS[0], g.pS[1]]

    def sp(self, e):
        pass

    def pool(self, e):
        pass

    def add_bias(self, e):
        wait(e, *self.x_read)
        for b in range(B):
            e.tensor_tensor(self.g.x[:, b, :], self.g.x[:, b, :], self.bo, ALU.add)\
                .then_inc(self.xb.sem, 1)

    def pe(self, e):
        g = self.g
        for sem, value in self.prev + self.w_loaded:
            wait(e, sem, value)
        for s in range(B + 1):
            if s < B:
                b = s
                if b >= 2:
                    wait(e, self.cx, b - 1)
                for c in range(KC):
                    mm = e.transpose(self.bT[b % 2][:, c * P:c * P + P], g.v[:, b, c * P:c * P + P],
                                     g.ident)
                mm.then_inc(self.t_full.sem, 1)
            b = s - 1
            if b >= 0:
                wait(e, self.cx, b + 1)
                if b >= 2:
                    wait(e, self.x, b - 1)
                for c in range(KC):
                    mm = e.matmul(self.bO[b % 2][:, 0:D], g.cx[:, b % 2, c * P:c * P + P],
                                  self.wo[:, c, :], start=c == 0, stop=c == KC - 1)
                mm.then_inc(self.o_full.sem, 1)

    def act(self, e):
        g = self.g
        for b in range(B):
            wait(e, self.t_full, b + 1)
            if b >= 2:
                wait(e, self.o_full, b - 1)
            e.activation(g.cx[:, b % 2, :], self.bT[b % 2][:, 0:D], ACT.Copy).then_inc(self.cx.sem, 1)

    def dve(self, e):
        g = self.g
        for b in range(B):
            wait(e, self.xb, b + 1)
            wait(e, self.o_full, b + 1)
            e.tensor_tensor(g.x[:, b, :], self.bO[b % 2][:, 0:D], g.x[:, b, :], ALU.add)\
                .then_inc(self.x.sem, 1)

    def drained(self):
        return [(self.x, B), (self.cx, B)]


class NormRows:

    def __init__(self, g, name, x_ready, eps, gamma, beta):
        self.g, self.x_ready, self.eps, self.gamma, self.beta = g, x_ready, eps, gamma, beta
        (self.stats, self.aggr, self.veps, self.rstd, self.h, self.scaled, self.x) = g.counts(
            "norm_rows", stats_ready=B, mean_var_ready=B, var_eps_ready=B, rstd_ready=B,
            normalised_ready=B, scaled_ready=B, x_ready=B)
        self.bn = g.st[:, 64:112].rearrange("p (b k) -> p b k", b=B)
        self.mv = g.st[:, 112:128].rearrange("p (b k) -> p b k", b=B)
        self.ve = g.st[:, 128:136]
        self.rs = g.st[:, 136:144]

    def sp(self, e):
        pass

    pe = act = sp

    def dve(self, e):
        g = self.g
        for b in range(B + 1):
            if b < B:
                wait(e, self.x_ready[0], self.x_ready[1](b))
                e.bn_stats(self.bn[:, b, :], g.x[:, b, :]).then_inc(self.stats.sem, 1)
                wait(e, self.stats, b + 1)
                e.bn_aggr(self.mv[:, b, :], self.bn[:, b, :]).then_inc(self.aggr.sem, 1)
            if b >= 1:
                c = b - 1
                wait(e, self.rstd, c + 1)
                e.tensor_scalar(g.x[:, c, :], g.x[:, c, :], self.mv[:, c, 0:1],
                                self.rs[:, c:c + 1], ALU.subtract, ALU.mult).then_inc(self.h.sem, 1)

    def pool(self, e):
        g = self.g
        for b in range(B):
            wait(e, self.aggr, b + 1)
            e.tensor_scalar(self.ve[:, b:b + 1], self.mv[:, b, 1:2], self.eps, None, ALU.add)\
                .then_inc(self.veps.sem, 1)
            wait(e, self.veps, b + 1)
            e.tensor_tensor(self.rs[:, b:b + 1], self.ve[:, b:b + 1], g.eps[:, 1:2], ALU.pow)\
                .then_inc(self.rstd.sem, 1)
            wait(e, self.h, b + 1)
            e.tensor_tensor(g.x[:, b, :], g.x[:, b, :], self.gamma, ALU.mult).then_inc(self.scaled.sem, 1)
            wait(e, self.scaled, b + 1)
            e.tensor_tensor(g.x[:, b, :], g.x[:, b, :], self.beta, ALU.add).then_inc(self.x.sem, 1)
            wait(e, self.x, b + 1)


class Mlp:

    def __init__(self, g, name, prev, func, b1, b2, x_read, ins_names, w_free):
        self.g, self.prev, self.func, self.b1, self.b2, self.x_read = g, prev, func, b1, b2, x_read
        self.ins_names, self.w_free = ins_names, w_free
        (self.w_loaded, self.xb, self.f_full, self.gelu, self.o_full, self.x) = g.counts(
            "mlp", weights_loaded=32, x_plus_bias_ready=B, hidden_in_bank=16,
            gelu_ready=16, output_in_bank=B, x_ready=B)
        self.gT = g.big[:, :].rearrange("p (f t) -> p f t", f=8)
        self.bO = [g.pS[0], g.pS[1], g.pT, g.pC]

    def sp(self, e):
        pass

    def load(self, e):
        g = self.g
        for sem, value in self.w_free:
            wait(e, sem, value)
        e.dma_start(g.w1[:, :, :], g.ins[self.ins_names[0]]).then_inc(self.w_loaded.sem, 16)
        e.dma_start(g.w2[:, :, :], g.ins[self.ins_names[1]]).then_inc(self.w_loaded.sem, 16)

    def pool(self, e):
        wait(e, *self.x_read)
        for b in range(B):
            e.tensor_tensor(self.g.x[:, b, :], self.g.x[:, b, :], self.b2, ALU.add)\
                .then_inc(self.xb.sem, 1)

    def pe(self, e):
        g = self.g
        for sem, value in self.prev:
            wait(e, sem, value)
        wait(e, self.w_loaded, 32)
        n = 0
        for half in range(2):
            for f in range(8):
                if n >= 4:
                    wait(e, self.gelu, n - 3)
                for c in range(KC):
                    mm = e.matmul(g.acc[n % 4][:, :], g.w1[:, c, f * P:f * P + P],
                                  g.hT[:, c, half * HALF:half * HALF + HALF],
                                  start=c == 0, stop=c == KC - 1)
                mm.then_inc(self.f_full.sem, 1)
                n += 1
        for b in range(B):
            wait(e, self.gelu, 8 if b < 4 else 16)
            if b >= 4:
                wait(e, self.x, b - 3)
            for f in range(8):
                mm = e.matmul(self.bO[b % 4][:, 0:D], self.gT[:, f, b * P:b * P + P], g.w2[:, f, :],
                              start=f == 0, stop=f == 7)
            mm.then_inc(self.o_full.sem, 1)

    def act(self, e):
        n = 0
        for half in range(2):
            for f in range(8):
                wait(e, self.f_full, n + 1)
                e.activation(self.gT[:, f, half * HALF:half * HALF + HALF], self.g.acc[n % 4][:, :],
                             self.func, bias=self.b1[:, f:f + 1]).then_inc(self.gelu.sem, 1)
                n += 1

    def dve(self, e):
        g = self.g
        for b in range(B):
            wait(e, self.xb, b + 1)
            wait(e, self.o_full, b + 1)
            e.tensor_tensor(g.x[:, b, :], self.bO[b % 4][:, 0:D], g.x[:, b, :], ALU.add)\
                .then_inc(self.x.sem, 1)

    def drained(self):
        return [(self.x, B), (self.gelu, 16)]


class CrossAttention:

    SCALE = 128 ** -0.5
    PACK = 3 * KC * D + 6

    def __init__(self, g, name, layer, prev, x_read, bo, w_free):
        self.g, self.layer, self.prev, self.x_read, self.bo = g, layer, prev, x_read, bo
        self.w_free = w_free
        (self.w_loaded, self.bv_loaded, self.wo_loaded, self.bvx, self.bk, self.xb,
         self.s_full, self.s_free, self.v_full, self.v_ready, self.t_full, self.pt, self.c_full,
         self.ctx, self.acc_done, self.max, self.nmax, self.rec, self.norm, self.x) = g.counts(
            "cross", pair_weights_loaded=16 * NPAIR, value_rows_loaded=16 * NPAIR,
            wo_loaded=16 * NPAIR, value_bias_ready=NPAIR, learnt_key_ready=2 * NPAIR,
            x_plus_bias_ready=B, s_bank_full=16 * NPAIR, s_bank_free_by_act=16 * NPAIR, values_in_bank=8 * NPAIR,
            values_ready=8 * NPAIR, t_bank_full=8 * NPAIR, probsT_ready=8 * NPAIR,
            c_bank_full=8 * NPAIR, ctx_ready=8 * NPAIR, acc_units_done=8 * NPAIR,
            max_ready=8 * NPAIR, negmax_ready=8 * NPAIR, recip_ready=8 * NPAIR,
            probs_normalised=8 * NPAIR, x_ready=B)
        self.w = g.wA[:, 0:3 * KC * D].rearrange("p (q c n) -> p q c n", q=3, c=KC)
        self.bias = g.wA[:, 3 * KC * D:self.PACK]
        self.wo = g.wB[:, 0:2 * D].rearrange("p (h n) -> p h n", h=2)
        self.bias_v = g.wB[:, 2 * D:2 * D + 2]
        self.qT = g.qT[:, :].rearrange("p (h t) -> p h t", h=2)
        self.kT = g.kT[:, :].rearrange("p (h b t) -> p h b t", h=2, b=B)
        self.E = g.E[:, :, 0:2 * (P + 1)].rearrange("p n (h t) -> p n h t", h=2)
        self.PT = g.PT[:, :, 0:D].rearrange("p n (h t) -> p n h t", h=2)
        self.st = g.st[:, 192:224].rearrange("p (k n h) -> p k n h", k=4, n=4)
        self.ring = Ring(["act"] * 16, 2)

    def sp(self, e):
        g, ins, at = self.g, self.g.ins, Layer0.at
        w, rows, wo = (ins[f"{k}{self.layer}"] for k in ("l2_w_", "l2_bv_", "l2_wo_"))

        def first(a):
            return a[0:1].rearrange("a p n -> (a p) n")

        for sem, value in self.w_free:
            wait(e, sem, value)
        bv = g.bv[:, :, :].rearrange("p k n -> p (k n)")
        e.dma_start(g.wA[:, 0:self.PACK], first(w)).then_inc(self.w_loaded.sem, 16)
        e.dma_start(bv, rows[0:1].broadcast_to([P, 2 * D])).then_inc(self.bv_loaded.sem, 16)
        e.dma_start(g.wB[:, :], first(wo)).then_inc(self.wo_loaded.sem, 16)
        with e.Fori(1, NPAIR) as p:
            wait(e, self.v_ready, 8 * p)
            e.dma_start(g.wA[:, 0:self.PACK], at(w, p)).then_inc(self.w_loaded.sem, 16)
            e.dma_start(bv, rows[bass.ds(p, 1)].broadcast_to([P, 2 * D])).then_inc(self.bv_loaded.sem, 16)
            wait(e, self.acc_done, 8 * p)
            e.dma_start(g.wB[:, :], at(wo, p)).then_inc(self.wo_loaded.sem, 16)

    def pe(self, e):
        g = self.g
        bank = g.pS

        def claim(n, p):
            need = self.ring.before(n, p)
            if need is not None:
                wait(e, self.s_free, need[1])

        def project_qk(p):
            wait(e, self.w_loaded, 16 * (p + 1))
            n = 0
            for q, src in enumerate((g.hT, g.cT)):
                for h in range(2):
                    for half in range(2):
                        claim(n, p)
                        for c in range(KC):
                            mm = e.matmul(bank[n % 2][:, :], self.w[:, q, c, h * P:h * P + P],
                                          src[:, c, half * HALF:half * HALF + HALF],
                                          start=c == 0, stop=c == KC - 1)
                        mm.then_inc(self.s_full.sem, 1)
                        n += 1

        def project_v(b, p):
            if b >= 2:
                wait(e, self.v_ready, 8 * p + b - 1)
            elif not (isinstance(p, int) and p == 0):
                wait(e, (self.pt, self.ctx)[b], 8 * p)
            for c in range(KC):
                mm = e.matmul((g.pT, g.pC)[b % 2][:, 0:D], g.cT[:, c, b * P:b * P + P],
                              self.w[:, 2, c, :], start=c == 0, stop=c == KC - 1)
            mm.then_inc(self.v_full.sem, 1)

        def scores(u, p):
            claim(8 + u, p)
            if u == 0:
                wait(e, self.s_free, 16 * p + 8)
                wait(e, self.bk, 2 * p + 2)
            for h in range(2):
                mm = e.matmul(bank[u % 2][:, h * (P + 1):(h + 1) * (P + 1)],
                              self.qT[:, h, u * P:u * P + P], self.kT[:, h, u, :],
                              start=True, stop=True)
            mm.then_inc(self.s_full.sem, 1)

        def transposes(u, p):
            wait(e, self.norm, 8 * p + u + 1)
            if u == 0:
                wait(e, self.v_ready, 8 * p + 7)
            if not (isinstance(p, int) and p == 0 and u == 0):
                wait(e, self.pt, 8 * p + u)
            for h in range(2):
                mm = e.transpose(g.pT[:, h * P:h * P + P], self.E[:, u % 4, h, 0:P], g.ident)
            mm.then_inc(self.t_full.sem, 1)

        def context(u, p):
            wait(e, self.pt, 8 * p + u + 1)
            if u == 0:
                wait(e, self.v_ready, 8 * p + 8)
            if not (isinstance(p, int) and p == 0 and u == 0):
                wait(e, self.ctx, 8 * p + u)
            for h in range(2):
                mm = e.matmul(g.pC[:, h * P:h * P + P], g.v[:, u, h * P:h * P + P],
                              self.PT[:, u % 2, h, :], start=True, stop=True)
            mm.then_inc(self.c_full.sem, 1)

        def output(u, p, first):
            wait(e, self.ctx, 8 * p + u + 1)
            if u == 0:
                wait(e, self.wo_loaded, 16 * (p + 1))
            for h in range(2):
                mm = e.matmul(g.acc[u // 2][:, (u % 2) * D:(u % 2) * D + D],
                              g.cx[:, u % 2, h * P:h * P + P], self.wo[:, h, :],
                              start=first and h == 0 and u % 2 == 0, stop=True,
                              skip_group_check=True)
            mm.then_inc(self.acc_done.sem, 1)

        def steps(slots, p, first):
            for s in slots:
                if s < B:
                    scores(s, p)
                if s < 2:
                    project_v(4 + 2 * s, p)
                    project_v(5 + 2 * s, p)
                if 0 <= s - 2 < B:
                    transposes(s - 2, p)
                if 0 <= s - 3 < B:
                    context(s - 3, p)
                if 0 <= s - 4 < B:
                    output(s - 4, p, first)

        for sem, value in self.prev:
            wait(e, sem, value)
        project_qk(0)
        for b in range(4):
            project_v(b, 0)
        steps(range(B), 0, True)

        def pair(p, first):
            steps(range(B, B + 1), p - 1, first)
            project_qk(p)
            steps(range(B + 1, B + 4), p - 1, first)
            for b in range(4):
                project_v(b, p)
            steps(range(B), p, False)

        pair(1, True)
        with e.Fori(2, NPAIR) as p:
            pair(p, False)
        steps(range(B, B + 4), NPAIR - 1, False)

    def act(self, e):
        g = self.g
        bank = g.pS

        def evacuate_qk(p):
            n = 0
            for q in range(2):
                for h in range(2):
                    for half in range(2):
                        wait(e, self.s_full, 16 * p + n + 1)
                        bias = self.bias[:, 2 * q + h:2 * q + h + 1]
                        if q == 0:
                            i = e.activation(self.qT[:, h, half * HALF:half * HALF + HALF],
                                             bank[n % 2][:, :], ACT.Identity, bias=bias)
                        else:
                            i = e.activation(self.kT[:, h, 4 * half:4 * half + 4, 0:P],
                                             bank[n % 2][:, :].rearrange("p (b t) -> p b t", b=4),
                                             ACT.Identity, bias=bias)
                        i.then_inc(self.s_free.sem, 1)
                        n += 1

        def exps(u, p):
            wait(e, self.nmax, 8 * p + u + 1)
            if not isinstance(p, int) or p > 0 or u >= 4:
                wait(e, self.t_full, 8 * p + u - 3)
                wait(e, self.norm, 8 * p + u - 3)
            for h in range(2):
                i = e.activation(self.E[:, u % 4, h, :], bank[u % 2][:, h * (P + 1):(h + 1) * (P + 1)],
                                 ACT.Exp, bias=self.st[:, 1, u % 4, h:h + 1], scale=self.SCALE,
                                 accum_out=self.st[:, 2, u % 4, h:h + 1])
            i.then_inc(self.s_free.sem, 1)

        def evacuate_t(u, p):
            wait(e, self.t_full, 8 * p + u + 1)
            e.activation(self.PT[:, u % 2], g.pT[:, 0:D].rearrange("p (h t) -> p h t", h=2),
                         ACT.Copy).then_inc(self.pt.sem, 1)

        def steps(slots, p):
            for s in slots:
                if s < B:
                    exps(s, p)
                if 0 <= s - 2 < B:
                    evacuate_t(s - 2, p)

        evacuate_qk(0)
        steps(range(B), 0)
        with e.Fori(1, NPAIR) as p:
            steps(range(B, B + 1), p - 1)
            evacuate_qk(p)
            steps(range(B + 1, B + 4), p - 1)
            steps(range(B), p)
        steps(range(B, B + 4), NPAIR - 1)

    def dve(self, e):
        g = self.g
        bank = g.pS
        bias_v = self.bias_v.unsqueeze(2).broadcast_to([P, 2, P])

        def evacuate_v(b, p):
            if b == 0:
                wait(e, self.bvx, p + 1)
                wait(e, self.bk, 2 * p + 2)
            wait(e, self.v_full, 8 * p + b + 1)
            e.tensor_tensor(g.v[:, b, :], (g.pT, g.pC)[b % 2][:, 0:D], g.bv[:, 0, :], ALU.add)\
                .then_inc(self.v_ready.sem, 1)

        def maxes(u, p):
            wait(e, self.s_full, 16 * p + 8 + u + 1)
            e.tensor_reduce(self.st[:, 0, u % 4, :], bank[u % 2][:, 0:2 * (P + 1)]
                            .rearrange("p (h t) -> p h t", h=2), AX.X, ALU.max).then_inc(self.max.sem, 1)
            wait(e, self.max, 8 * p + u + 1)
            e.tensor_scalar(self.st[:, 1, u % 4, :], self.st[:, 0, u % 4, :], -self.SCALE, None,
                            ALU.mult).then_inc(self.nmax.sem, 1)

        def normalise(u, p):
            wait(e, self.s_free, 16 * p + 8 + u + 1)
            e.reciprocal(self.st[:, 3, u % 4, :], self.st[:, 2, u % 4, :]).then_inc(self.rec.sem, 1)
            wait(e, self.rec, 8 * p + u + 1)
            e.tensor_tensor(self.E[:, u % 4, :, 0:P], self.E[:, u % 4, :, 0:P],
                            self.st[:, 3, u % 4, :].unsqueeze(2).broadcast_to([P, 2, P]),
                            ALU.mult).then_inc(self.norm.sem, 1)

        def evacuate_c(u, p):
            wait(e, self.c_full, 8 * p + u + 1)
            if u == 0:
                wait(e, self.wo_loaded, 16 * (p + 1))
            if not (isinstance(p, int) and p == 0 and u < 2):
                wait(e, self.acc_done, 8 * p + u - 1)
            e.tensor_tensor(g.cx[:, u % 2, :].rearrange("p (h t) -> p h t", h=2),
                            g.pC[:, 0:D].rearrange("p (h t) -> p h t", h=2), bias_v, ALU.add)\
                .then_inc(self.ctx.sem, 1)

        def steps(slots, p):
            for s in slots:
                if s < B:
                    maxes(s, p)
                if s < 2:
                    evacuate_v(4 + 2 * s, p)
                if 0 <= s - 1 < B:
                    normalise(s - 1, p)
                if s < 2:
                    evacuate_v(5 + 2 * s, p)
                if 0 <= s - 3 < B:
                    evacuate_c(s - 3, p)

        def pair(p):
            for b in range(4):
                evacuate_v(b, p)
            steps(range(B), p)

        pair(0)
        with e.Fori(1, NPAIR) as p:
            steps(range(B, B + 4), p - 1)
            pair(p)
        steps(range(B, B + 4), NPAIR - 1)
        for b in range(B):
            wait(e, self.xb, b + 1)
            wait(e, self.acc_done, 8 * (NPAIR - 1) + 2 * (b // 2) + 2)
            e.tensor_tensor(g.x[:, b, :], g.acc[b // 2][:, (b % 2) * D:(b % 2) * D + D],
                            g.x[:, b, :], ALU.add).then_inc(self.x.sem, 1)

    def pool(self, e):
        g = self.g

        def prepare(p):
            wait(e, self.w_loaded, 16 * (p + 1))
            if not (isinstance(p, int) and p == 0):
                wait(e, self.s_full, 16 * p)
            wait(e, self.bv_loaded, 16 * (p + 1))
            e.tensor_tensor(g.bv[:, 0, :], g.bv[:, 0, :], g.bv[:, 1, :], ALU.subtract)\
                .then_inc(self.bvx.sem, 1)
            for h in range(2):
                e.tensor_copy(self.kT[:, h, :, P], self.bias[:, 4 + h:5 + h].broadcast_to([P, B]))\
                    .then_inc(self.bk.sem, 1)

        for sem, value in self.prev:
            wait(e, sem, value)
        prepare(0)
        wait(e, *self.x_read)
        for b in range(B):
            e.tensor_tensor(g.x[:, b, :], g.x[:, b, :], self.bo, ALU.add).then_inc(self.xb.sem, 1)
        with e.Fori(1, NPAIR) as p:
            prepare(p)

    def drained(self):
        return [(self.x, B)]


def store(g, e, ready, base):
    done = g.sem("stored")
    for b in range(B):
        wait(e, ready, base[b])
        e.dma_start(g.out[b], g.x[:, b, :]).then_inc(done, 16)
    e.wait_ge(done, 16 * B)


def build_program(nc, ins, out, stop=None):
    with ExitStack() as ctx:
        g = Shared(nc, ctx, ins)
        g.out = out
        stages, last = plan(g, stop)
        block = ctx.enter_context(nc.Block())

        @block.sync
        def _(e):
            for s in stages:
                s.sp(e)
            store(g, e, *last)

        @block.tensor
        def _(e):
            for s in stages:
                s.pe(e)

        @block.scalar
        def _(e):
            for s in stages:
                s.act(e)

        @block.vector
        def _(e):
            for s in stages:
                s.dve(e)

        @block.gpsimd
        def _(e):
            for s in stages:
                s.pool(e)


class Loads:

    def __init__(self, g, name, loads, free=()):
        self.g, self.loads, self.free = g, loads, free
        self.sem = g.sem(f"{name}_loaded")

    def sp(self, e):
        for sem, value in self.free:
            wait(e, sem, value)
        for dst, src in self.loads:
            e.dma_start(dst, src).then_inc(self.sem, 16)

    def pe(self, e):
        pass

    act = dve = pool = pe

    def done(self):
        return [(self.sem, 16 * len(self.loads))]


class AdditiveMask:

    def __init__(self, g, name, loaded, free):
        self.g, self.loaded, self.free = g, loaded, free
        self.sem = g.sem(f"{name}_amask_ready")

    def pool(self, e):
        for sem, value in self.loaded + self.free:
            wait(e, sem, value)
        e.tensor_scalar(self.g.amask[:, :, :], self.g.mask[:, :, :], -1.0, 10000.0, ALU.add, ALU.mult)\
            .then_inc(self.sem, 1)

    def pe(self, e):
        pass

    act = dve = sp = pe

    def done(self):
        return [(self.sem, 1)]


def plan(g, stop):
    ins, col, row = g.ins, g.col, g.row
    by_batch = lambda sem: (sem, lambda b: b + 1)

    w1 = g.w1[:, :, :].rearrange("p c n -> p (c n)")
    l1_loads = Loads(g, "l1", [(w1[:, 0:1792], ins["l1_w"]), (g.mask[:, :, :], ins["mask0"])])
    l0 = Layer0(g)
    stages = [l1_loads, l0]
    x_l0 = (l0.x_done, lambda b: 2 * (b // 2) + 2)
    l0_end = [(l0.x_done, 8), (l0.f_sd, 4)]
    if stop and stop[0] == "0":
        return stages, (x_l0[0], [x_l0[1](b) for b in range(B)])

    wq, wk = (w1[:, i:i + 512].rearrange("p (c n) -> p c n", c=KC) for i in (0, 512))
    wv = w1[:, 1024:1280].rearrange("p (c n) -> p c n", c=KC)
    wo = w1[:, 1280:1792].rearrange("p (c n) -> p c n", c=KC)
    t1 = NormT(g, "transpose_l1", g.hT, x_l0, l0_end)
    p1 = Project(g, "l1_p", t1.drained(), l1_loads.done(), g.hT, g.cT, wq, wk, wv, col("l1_bq"),
                 col("l1_bk"), row("l1_bv"), 1)
    a1 = SmallHeads(g, "l1_a", p1.drained(), 8, 8 ** -0.5, False, l1_loads.done())
    o1 = OutProject(g, "l1_o", a1.drained(), 8, wo, row("l1_bo"), t1.read_x(), [])
    n1 = NormRows(g, "l1_n", by_batch(o1.x), 1e-6, row("l1_gamma"), row("l1_beta"))
    stages += [t1, p1, BiasAhead(o1), a1, o1, n1]
    if stop and stop[0] == "1":
        return stages, (n1.x, list(range(1, B + 1)))

    masks = Loads(g, "l3_masks", [(g.mask[:, 0, :], ins["mask1"])], a1.drained())
    t2 = NormT(g, "l2_t1", g.hT, by_batch(n1.x), o1.drained(), (col("l2_ln1_scale"), col("l2_ln1_offset")))
    a2 = CrossAttention(g, "l2_a1", 0, t2.drained(), t2.read_x(), row("l2_bo1"),
                        [(l0.acc_done, 64)])
    t3 = NormT(g, "l2_t2", g.hT, by_batch(a2.x), a2.drained(), (col("l2_ln2_scale"), col("l2_ln2_offset")))
    a3 = CrossAttention(g, "l2_a2", 1, t3.drained(), t3.read_x(), row("l2_bo2"),
                        [(a2.acc_done, 64)])
    t4 = NormT(g, "l2_t3", g.hT, by_batch(a3.x), a3.drained(),
               (col("l2_ln_mlp_scale"), col("l2_ln_mlp_offset")))
    m2 = Mlp(g, "l2_m", t4.drained(), ACT.Gelu, col("l2_b_fc1"), row("l2_b_fc2"), t4.read_x(),
             ("l2_w1", "l2_w2"), o1.drained())
    stages += [masks, t2, MlpLoads(m2), a2, t3, a3, t4, m2]
    if stop and stop[0] == "2":
        return stages, (m2.x, list(range(1, B + 1)))

    wa = g.wA[:, :]
    wc = g.wC[:, :]
    s_loads = Loads(g, "l3_self", [(wa, ins["l3_self"])], [(a3.acc_done, 64)])
    c_loads = Loads(g, "l3_cross", [(wc, ins["l3_cross"])])
    am1 = AdditiveMask(g, "l3_self", masks.done(), [])
    three = lambda w, n: w[:, 0:KC * n].rearrange("p (c n) -> p c n", c=KC)
    wqkv, wao = three(wa, 3 * D), wa[:, 1536:2048].rearrange("p (c n) -> p c n", c=KC)
    wq3, wkv3 = three(wc, D), wc[:, 512:1536].rearrange("p (c n) -> p c n", c=KC)
    wco = wc[:, 1536:2048].rearrange("p (c n) -> p c n", c=KC)
    t5 = NormT(g, "l3_t1", g.hT, by_batch(m2.x), m2.drained(), (col("l3_ln1_s"), col("l3_ln1_b")))
    p5 = Project(g, "l3_p1", t5.drained(), s_loads.done(), g.hT, g.hT, wqkv[:, :, 0:D],
                 wqkv[:, :, D:2 * D], wqkv[:, :, 2 * D:3 * D], col("l3_bq"), col("l3_bk"),
                 row("l3_bv"), 4)
    a5 = SmallHeads(g, "l3_a1", p5.drained(), 16, 0.25, True, masks.done() + am1.done())
    a5.one_mask = True
    o5 = OutProject(g, "l3_o1", a5.drained(), 16, wao, row("l3_b_ao"), t5.read_x(), [])
    masks2 = Loads(g, "l3_masks2", [(g.mask[:, :, :], ins["mask2"])], a5.drained())
    am2 = AdditiveMask(g, "l3_cross", masks2.done(), a5.drained())
    t6 = NormT(g, "l3_t2", g.hT, by_batch(o5.x), o5.drained(), (col("l3_ln2_s"), col("l3_ln2_b")))
    p6 = Project(g, "l3_p2", t6.drained(), c_loads.done(), g.hT, g.cT, wq3, wkv3[:, :, 0:D],
                 wkv3[:, :, D:2 * D], col("l3_bq2"), col("l3_bk2"), row("l3_bv2"), 4)
    a6 = SmallHeads(g, "l3_a2", p6.drained(), 16, 0.25, True, masks2.done() + am2.done())
    o6 = OutProject(g, "l3_o2", a6.drained(), 16, wco, row("l3_b_co"), t6.read_x(), [])
    t7 = NormT(g, "l3_t3", g.hT, by_batch(o6.x), o6.drained(), (col("l3_ln3_s"), col("l3_ln3_b")))
    m3 = Mlp(g, "l3_m", t7.drained(), ACT.Gelu_apprx_tanh, col("l3_b1"), row("l3_b2"), t7.read_x(),
             ("l3_w1", "l3_w2"), [(m2.x, B)])
    stages += [s_loads, c_loads, MlpLoads(m3), am1, t5, p5, BiasAhead(o5), a5, o5, masks2, am2, t6, p6,
               BiasAhead(o6), a6, o6, t7, m3]
    return stages, (m3.x, list(range(1, B + 1)))


class BiasAhead:

    def __init__(self, stage):
        self.stage = stage

    def pool(self, e):
        self.stage.add_bias(e)

    def pe(self, e):
        pass

    act = dve = sp = pe


class MlpLoads:

    def __init__(self, mlp):
        self.mlp = mlp

    def sp(self, e):
        self.mlp.load(e)

    def pe(self, e):
        pass

    act = dve = pool = pe


def layout(a):
    f = {k: np.asarray(v) for k, v in a.items()}
    c = np.ascontiguousarray
    out = {}
    out["x_dbl"] = c(f["x"].transpose(1, 0, 2).reshape(P, B * D))
    out["ctx_dbl"] = c(f["ctx_2048"].transpose(1, 0, 2).reshape(P, B * D))
    out["ctxT"] = c(f["ctx_2048"].reshape(T, KC, P).transpose(2, 1, 0))
    w = np.stack([f["L0_xattn_Wqkv0"], f["L0_xattn_Winj0"], f["L0_xattn_Wqkv1"], f["L0_xattn_Winj1"]])
    w = w.reshape(4, 3, NPAIR, P, P).transpose(2, 4, 1, 0, 3).reshape(NPAIR, P, 12 * P)
    rwb = f["L0_xattn_r_w_bias"].reshape(NPAIR, P, 1)
    out["l0_w"] = c(np.concatenate([w, rwb], axis=2))
    out["l0_wo"] = c(f["L0_xattn_Wo"].reshape(P, NPAIR, P).transpose(1, 2, 0))
    tiles = lambda w: w.reshape(-1, P, w.shape[1]).transpose(1, 0, 2)
    flat = lambda w: w.reshape(P, -1)
    wk = np.broadcast_to(f["L1_xattn_Wk"].reshape(D, 8, 1, 8), (D, 8, 4, 8)).reshape(D, D)
    bk = np.broadcast_to(f["L1_xattn_bk"].reshape(8, 1, 8), (8, 4, 8)).reshape(D)
    wv = np.concatenate([f["L1_xattn_Wv"], np.zeros((D, 64), np.float32)], axis=1)
    out["l1_w"] = c(np.concatenate([flat(tiles(f["L1_xattn_Wq"])), flat(tiles(wk)), flat(tiles(wv)),
                                    flat(tiles(f["L1_xattn_Wo"]))], axis=1))
    w, wo, rows = [], [], []
    for i in "12":
        n = lambda name: f[f"L2_xattn_{name}{i}"]
        m = np.stack([n("wq"), n("wk"), n("wv")]).reshape(3, KC, P, NPAIR, D)
        m = m.transpose(3, 2, 0, 1, 4).reshape(NPAIR, P, 3 * KC * D)
        bias = np.stack([n(k).reshape(NPAIR, 2, P) for k in ("bq", "bk", "bias_k")])
        w.append(np.concatenate([m, bias.transpose(1, 3, 0, 2).reshape(NPAIR, P, 6)], axis=2))
        m = n("wo").reshape(NPAIR, 2, P, D).transpose(0, 2, 1, 3).reshape(NPAIR, P, 2 * D)
        wo.append(np.concatenate([m, n("bias_v").reshape(NPAIR, 2, P).transpose(0, 2, 1)], axis=2))
        rows.append(np.stack([n("bv").reshape(NPAIR, D), n("bias_v").reshape(NPAIR, D)], axis=1)
                    .reshape(NPAIR, 2 * D))
    for i in range(2):
        out[f"l2_w_{i}"], out[f"l2_wo_{i}"], out[f"l2_bv_{i}"] = c(w[i]), c(wo[i]), c(rows[i])
    out["l2_w1"], out["l2_w2"] = c(tiles(f["L2_xattn_w_fc1"])), c(tiles(f["L2_xattn_w_fc2"]))
    out["l3_self"] = c(np.concatenate([flat(tiles(f["L3_xattn_w_qkv"])),
                                       flat(tiles(f["L3_xattn_w_ao"]))], axis=1))
    out["l3_cross"] = c(np.concatenate([flat(tiles(f["L3_xattn_w_q"])), flat(tiles(f["L3_xattn_w_kv"])),
                                        flat(tiles(f["L3_xattn_w_co"]))], axis=1))
    out["l3_w1"], out["l3_w2"] = c(tiles(f["L3_xattn_w1"])), c(tiles(f["L3_xattn_w2"]))
    out["mask0"] = c(f["mask_Bx1xSxS2_ff0"][:, 0].transpose(1, 0, 2))
    out["mask1"] = c(f["mask_1x1xSxS2_fc1"][0, 0])
    out["mask2"] = c(f["mask_Bx1xSxS2_ff1"][:, 0].transpose(1, 0, 2))
    b_qkv, b_kv = f["L3_xattn_b_qkv"], f["L3_xattn_b_kv"]
    rows = {"l1_bv": np.concatenate([f["L1_xattn_bv"], np.zeros(D - 64, np.float32)]),
            "l3_bv": b_qkv[2 * D:], "l3_bv2": b_kv[D:]}
    cols = {"l1_bk": bk, "l3_bq": b_qkv[0:D], "l3_bk": b_qkv[D:2 * D], "l3_bq2": f["L3_xattn_b_q"],
            "l3_bk2": b_kv[0:D]}
    named = lambda name: f[name[0:2].upper() + "_xattn" + name[2:]]
    out["rows"] = c(np.concatenate([rows[n] if n in rows else named(n) for n in ROWS]).reshape(1, -1))
    out["cols"] = c(np.concatenate([(cols[n] if n in cols else named(n)).reshape(-1, P).T
                                    for n in COLS], axis=1))
    row = np.arange(P)[:, None]
    out["consts"] = np.concatenate([
        np.eye(P, dtype=np.float32), np.full((P, P), 1.0 / P, np.float32),
        (row // 8 == np.arange(16)[None, :]).astype(np.float32),
        (row // 16 == np.arange(8)[None, :]).astype(np.float32)], axis=1)
    return out


def kernel(**inputs):
    import concourse.bacc as bacc
    from concourse.bass_utils import run_bass_kernel_spmd

    nc = bacc.Bacc("TRN2", target_bir_lowering=False, num_devices=1)
    arrays = layout(inputs)
    ins = {k: nc.dram_tensor("in_" + k, a.shape, F32, kind="ExternalInput").ap() for k, a in arrays.items()}
    out = nc.dram_tensor("out", (B, P, D), F32, kind="ExternalOutput").ap()
    build_program(nc, ins, out)
    r = run_bass_kernel_spmd(nc, [{"in_" + k: a for k, a in arrays.items()}], core_ids=[0])
    return r.results[0]["out"]
```

```python
from contextlib import ExitStack

import numpy as np

import concourse.bass as bass
from concourse import mybir

F32 = mybir.dt.float32
F32R = mybir.dt.float32r
ALU = mybir.AluOpType
ACT = mybir.ActivationFunctionType
AX = mybir.AxisListType

P = 128
B = 8
D = 256
KC = D // P
T = B * P
NPAIR = 8
HALF = T // 2


ROWS = ["l1_bv", "l1_bo", "l1_gamma", "l1_beta", "l2_bo1", "l2_bo2", "l2_b_fc2",
        "l3_bv", "l3_b_ao", "l3_bv2", "l3_b_co", "l3_b2"]
COLS = {}
NCOLS = 0
for _name, _n in [("l0_bo", 1), ("l1_bq", 2), ("l1_bk", 2),
                  ("l2_ln1_scale", 2), ("l2_ln1_offset", 2), ("l2_ln2_scale", 2), ("l2_ln2_offset", 2),
                  ("l2_ln_mlp_scale", 2), ("l2_ln_mlp_offset", 2), ("l2_b_fc1", 8),
                  ("l3_ln1_s", 2), ("l3_ln1_b", 2), ("l3_bq", 2), ("l3_bk", 2),
                  ("l3_ln2_s", 2), ("l3_ln2_b", 2), ("l3_bq2", 2), ("l3_bk2", 2),
                  ("l3_ln3_s", 2), ("l3_ln3_b", 2), ("l3_b1", 8)]:
    COLS[_name] = (NCOLS, _n)
    NCOLS += _n


class Shared:

    def __init__(self, nc, ctx, ins):
        self.nc, self.ctx, self.ins = nc, ctx, ins
        self.shared = {}

        def sb(name, shape, dtype=F32):
            return ctx.enter_context(nc.sbuf_tensor(name, shape, dtype))

        def alias(parts, size, name, shape):
            with ExitStack() as inner:
                out = [inner.enter_context(nc.sbuf_tensor(n, dims, F32)) for n, dims in parts]
            out.append(sb(name, shape, F32R))
            if size > int(np.prod(shape[1:])):
                sb(name + "_rest", [P, size - int(np.prod(shape[1:]))])
            return out

        self.big, self.split = alias([("big", [P, 8192])], 8192, "split_sources", [P, 2, 2, KC, T])
        self.w2, self.wC, self.kz_hi = alias([("w_fc2", [P, 8, D]), ("weights_c", [P, 2048])], 4096,
                                             "l0_keys_high", [P, 4096])
        self.sm, self.km, self.bv, self.kz_lo = alias(
            [("masked_scores", [P, 4, 512]), ("masked_keys", [P, 3, 512]),
             ("value_bias_rows", [P, 2, D])], 4096, "l0_keys_low", [P, 4096])
        self.qT, self.kT, self.q_parts = alias(
            [("qT", [P, 2 * T]), ("kT", [P, 2 * B * (P + 1)])], 2 * T + 2 * B * (P + 1),
            "l0_queries_parts", [P, 2, 2 * T])
        self.wS = sb("split_pair_weights", [P, 2, 3 * KC * D], F32R)
        self.x = sb("x_residual", [P, B, D])
        self.hT = sb("hT", [P, KC, T])
        self.cT = sb("ctxT", [P, KC, T])
        self.v = sb("v", [P, B, D])
        self.E = sb("probs", [P, 4, 1024])
        self.PT = sb("probsT", [P, 2, 1024])
        self.cx = sb("ctx_small", [P, 2, D])
        self.hn = sb("normalised", [P, 4, D])
        self.wA = sb("weights_a", [P, 2048])
        self.wB = sb("weights_b", [P, 2 * D + 2])
        self.w1 = sb("w_fc1", [P, KC, 1024])
        self.rows = sb("bias_rows", [P, len(ROWS), D])
        self.mask = sb("mask", [P, B, P])
        self.amask = sb("additive_mask", [P, B, P])
        self.st = sb("stats", [P, 256])
        self.cols = sb("bias_cols", [P, NCOLS])
        self.eps = sb("eps", [P, 2])
        self.consts = sb("consts", [P, 128 + 128 + 16 + 8])
        self.ident = self.consts[:, 0:128]
        self.mean_mat = self.consts[:, 128:256]
        self.head8 = self.consts[:, 256:272]
        self.head16 = self.consts[:, 272:280]
        self.acc = [ctx.enter_context(nc.psum_tensor(f"acc{i}", [P, 512], F32)) for i in range(4)]
        self.pS = [ctx.enter_context(nc.psum_tensor(f"pS{i}", [P, 512], F32)) for i in range(2)]
        self.pT = ctx.enter_context(nc.psum_tensor("pT", [P, 512], F32))
        self.pC = ctx.enter_context(nc.psum_tensor("pC", [P, 512], F32))

    def row(self, name):
        return self.rows[:, ROWS.index(name), :]

    def col(self, name):
        at, n = COLS[name]
        return self.cols[:, at:at + n]

    def counts(self, kind, **totals):
        out = []
        for name, total in totals.items():
            if (kind, name) not in self.shared:
                self.shared[kind, name] = [self.sem(f"{kind}_{name}"), 0]
            entry = self.shared[kind, name]
            out.append(Count(*entry))
            entry[1] += total
        return out

    def sem(self, name):
        return self.ctx.enter_context(self.nc.semaphore(name))


class Count:

    def __init__(self, sem, base):
        self.sem, self.base = sem, base


def wait(e, count, value):
    if isinstance(count, Count):
        e.wait_ge(count.sem, count.base + value)
    else:
        e.wait_ge(count, value)


class Ring:

    def __init__(self, kinds, depth):
        self.kinds, self.depth = kinds, depth

    def before(self, n, i):
        m = n - self.depth
        if m < 0:
            if isinstance(i, int) and i == 0:
                return None
            m, i = m + len(self.kinds), i - 1
        kind = self.kinds[m]
        return kind, i * self.kinds.count(kind) + self.kinds[:m + 1].count(kind)


PAIRS = [(0, 0), (0, 1), (1, 0)]
PARTS = [(c, *pair) for c in range(KC) for pair in PAIRS]


class Layer0:

    SCALE = 64 ** -0.5
    QK = [(q, half, chunk) for q in range(2) for half in range(2) for chunk in range(2)]
    PACK = 12 * P + 1

    def __init__(self, g):
        self.g = g
        s = g.sem
        self.z_loaded = s("l0_z_loaded")
        self.u_loaded = s("l0_u_loaded")
        self.consts_loaded = s("l0_consts_loaded")
        self.rest_loaded = s("l0_biases_and_context_loaded")
        self.w_loaded = s("l0_pair_weights_loaded")
        self.wo_loaded = s("l0_wo_loaded")
        self.consts_set = s("l0_key_zeros_set")
        self.s_full = s("l0_s_bank_full")
        self.s_free = s("l0_s_bank_free_by_act")
        self.src_hi = s("l0_inputs_high_ready")
        self.src_lo = s("l0_inputs_low_ready")
        self.w_hi = s("l0_weights_high_ready")
        self.w_lo = s("l0_weights_low_ready")
        self.qk_hi = s("l0_q_k_high_ready")
        self.qk_lo = s("l0_q_k_low_ready")
        self.v_full = s("l0_values_in_bank")
        self.v_ready = s("l0_values_ready")
        self.t_full = s("l0_t_bank_full")
        self.pt0 = s("l0_probsT_half0_ready")
        self.pt1 = s("l0_probsT_half1_ready")
        self.c_full = s("l0_c_bank_full")
        self.ctx = s("l0_ctx_ready")
        self.acc_done = s("l0_acc_units_done")
        self.nmax = s("l0_negmax_ready")
        self.rec = s("l0_recip_ready")
        self.norm0 = s("l0_probs_half0_normalised")
        self.norm1 = s("l0_probs_half1_normalised")
        self.f_x = s("l0_sum_ready")
        self.f_mean = s("l0_mean_ready")
        self.f_xc = s("l0_centered_ready")
        self.f_sq = s("l0_square_ready")
        self.f_var = s("l0_var_ready")
        self.f_sd = s("l0_std_ready")
        self.f_rs = s("l0_rstd_ready")
        self.x_done = s("l0_output_ready")
        self.z = g.x[:, :, :]
        self.u = g.hT[:, :, :].rearrange("p c t -> p (c t)").rearrange("p (b l) -> p b l", b=B)
        flat = [[g.split[:, m, k, :, :].rearrange("p c t -> p (c t)") for k in range(2)] for m in range(2)]
        self.zu = [[a.rearrange("p (b l) -> p b l", b=B) for a in parts] for parts in flat]
        self.kz = [a[:, :].rearrange("p (b h l) -> p b h l", b=B, h=2) for a in (g.kz_hi, g.kz_lo)]
        self.q = [g.q_parts[:, k, :].rearrange("p (b l) -> p b l", b=B) for k in range(2)]
        self.v = g.v[:, :, :].rearrange("p b (j n) -> p b j n", j=2)
        self.w = g.wA[:, 0:12 * P].rearrange("p (q m o) -> p q m o", q=3, m=4)
        self.ws = [g.wS[:, k, 0:8 * P].rearrange("p (q m o) -> p q m o", q=2, m=4) for k in range(2)]
        self.rwb = g.wA[:, 12 * P:12 * P + 1]
        self.wo = g.wB[:, 0:P]
        self.E = g.E[:, :, :].rearrange("p n (i h l) -> p n i h l", i=2, h=2)
        self.PT = g.PT[:, :, :].rearrange("p n (j h l) -> p n j h l", j=2, h=2)
        self.st = g.st[:, 0:64].rearrange("p (k n i h) -> p k n i h", k=4, n=4, i=2)
        self.bo = g.col("l0_bo")
        self.eps = g.eps[:, 0:1]

    def load_inputs(self, e):
        g, ins = self.g, self.g.ins
        e.dma_start(g.wA[:, 0:self.PACK], ins["l0_w"][0]).then_inc(self.w_loaded, 16)
        e.dma_start(self.z, ins["x_dbl"].rearrange("p (b l) -> p b l", b=B)).then_inc(self.z_loaded, 16)
        e.dma_start(self.u, ins["ctx_dbl"].rearrange("p (b l) -> p b l", b=B)).then_inc(self.u_loaded, 16)
        e.dma_start(g.consts[:, :], ins["consts"]).then_inc(self.consts_loaded, 16)
        e.dma_start(self.wo, ins["l0_wo"][0]).then_inc(self.wo_loaded, 16)
        e.dma_start(g.cols[:, :], ins["cols"]).then_inc(self.rest_loaded, 16)
        e.dma_start(g.cT[:, :, :], ins["ctxT"]).then_inc(self.rest_loaded, 16)
        e.dma_start(g.rows[:, :, :].rearrange("p r n -> p (r n)"),
                    ins["rows"].broadcast_to([P, len(ROWS) * D])).then_inc(self.rest_loaded, 16)

    def sp(self, e):
        g, ins = self.g, self.g.ins

        def pair(p):
            e.wait_ge(self.v_ready, 8 * p)
            e.wait_ge(self.qk_lo, 8 * p)
            e.dma_start(g.wA[:, 0:self.PACK], self.at(ins["l0_w"], p)).then_inc(self.w_loaded, 16)
            e.wait_ge(self.acc_done, 8 * p)
            e.dma_start(self.wo, self.at(ins["l0_wo"], p)).then_inc(self.wo_loaded, 16)

        with e.Fori(1, NPAIR) as p:
            pair(p)

    @staticmethod
    def at(array, p):
        return array[bass.ds(p, 1)].rearrange("a p n -> (a p) n")

    def pe(self, e):
        g = self.g
        ring = Ring(["dve"] * 8 + ["act"] * 16, 2)
        bank = g.pS

        def claim(n, p):
            need = ring.before(n, p)
            if need is not None:
                e.wait_ge({"dve": self.qk_lo, "act": self.s_free}[need[0]], need[1])

        def project_qk(p, groups=range(8)):
            if groups[0] == 0:
                e.wait_ge(self.w_lo, 4 * (p + 1))
            for n in groups:
                q, half, chunk = self.QK[n]
                claim(n, p)
                if isinstance(p, int) and p == 0 and n < 3:
                    e.wait_ge(self.src_lo, 4 if n < 2 else 8)
                bs, ls = slice(4 * half, 4 * half + 4), slice(chunk * P, chunk * P + P)
                for i, (m, kw, ks) in enumerate(PARTS):
                    mm = e.matmul(bank[n % 2][:, :], self.ws[kw][:, q, 2 * chunk + m, :],
                                  self.zu[m][ks][:, bs, ls], start=i == 0, stop=i == len(PARTS) - 1)
                mm.then_inc(self.s_full, 1)

        def project_v(b, p):
            if b >= 2:
                e.wait_ge(self.v_ready, 8 * p + b - 1)
            elif not (isinstance(p, int) and p == 0):
                e.wait_ge((self.pt1, self.ctx)[b], 8 * p)
            for j in range(2):
                for m, src in enumerate((self.z, self.u)):
                    mm = e.matmul((g.pT, g.pC)[b % 2][:, j * P:j * P + P], src[:, b, j * P:j * P + P],
                                  self.w[:, 2, 2 * j + m, :], start=m == 0, stop=m == 1)
            mm.then_inc(self.v_full, 1)

        def scores(u, it, p):
            claim(8 + 2 * u + it, p)
            if (u, it) == (0, 0):
                e.wait_ge(self.qk_lo, 8 * p + 8)
            for i, (kq, kk) in enumerate(PAIRS):
                mm = e.matmul(bank[it][:, :], self.q[kq][:, u, it * P:it * P + P],
                              self.kz[kk][:, u, :, :], start=i == 0, stop=i == len(PAIRS) - 1)
            mm.then_inc(self.s_full, 1)

        def transposes(u, jt, p):
            if jt == 0:
                e.wait_ge(self.norm0, 8 * p + u + 1)
                e.wait_ge(self.norm1, 8 * p + u + 1)
                if u == 0:
                    e.wait_ge(self.v_ready, 8 * p + 7)
                if not (isinstance(p, int) and p == 0 and u == 0):
                    e.wait_ge(self.pt1, 8 * p + u)
            else:
                e.wait_ge(self.pt0, 8 * p + u + 1)
            for h in range(2):
                for it in range(2):
                    mm = e.transpose(g.pT[:, (2 * h + it) * P:(2 * h + it + 1) * P],
                                     self.E[:, u % 4, it, h, jt * P:jt * P + P], g.ident)
            mm.then_inc(self.t_full, 1)

        def context(u, h, p):
            if h == 0:
                if u == 0:
                    e.wait_ge(self.v_ready, 8 * p + 8)
                e.wait_ge(self.pt0, 8 * p + u + 1)
                e.wait_ge(self.pt1, 8 * p + u + 1)
                if not (isinstance(p, int) and p == 0 and u == 0):
                    e.wait_ge(self.ctx, 8 * p + u)
            for j in range(2):
                mm = e.matmul(g.pC[64 * h:64 * h + 64, 0:D], self.v[:, u, j, 64 * h:64 * h + 64],
                              self.PT[:, u % 2, j, h, :], start=j == 0, stop=j == 1)
            if h == 1:
                mm.then_inc(self.c_full, 1)

        def output(u, p, first):
            e.wait_ge(self.ctx, 8 * p + u + 1)
            if u == 0:
                e.wait_ge(self.wo_loaded, 16 * (p + 1))
            e.matmul(g.acc[u // 2][:, (u % 2) * D:(u % 2) * D + D], self.wo, g.cx[:, u % 2, :],
                     start=first and u % 2 == 0, stop=True, skip_group_check=True)\
                .then_inc(self.acc_done, 1)

        def steps(slots, p, first):
            for s in slots:
                for it in range(2):
                    if s < B:
                        scores(s, it, p)
                    if s < 2:
                        project_v(4 + 2 * s + it, p)
                    if 0 <= s - 2 < B:
                        transposes(s - 2, it, p)
                    if 0 <= s - 3 < B:
                        context(s - 3, it, p)
                if 0 <= s - 4 < B:
                    output(s - 4, p, first)

        for sem in (self.w_loaded, self.z_loaded, self.u_loaded):
            e.wait_ge(sem, 16)
        for b in range(4):
            project_v(b, 0)
        project_qk(0)
        e.wait_ge(self.consts_loaded, 16)
        e.wait_ge(self.consts_set, 6)
        steps(range(B), 0, True)

        def pair(p, first):
            for t in range(4):
                steps([B + t], p - 1, first)
                project_qk(p, [2 * t, 2 * t + 1])
            for b in range(4):
                project_v(b, p)
            steps(range(B), p, False)

        e.wait_ge(self.rest_loaded, 48)
        pair(1, True)
        with e.Fori(2, NPAIR) as p:
            pair(p, False)
        steps(range(B, B + 4), NPAIR - 1, False)
        for c in range(4):
            e.wait_ge(self.f_x, c + 1)
            e.matmul(g.acc[c][:, :], g.mean_mat, self.xs(c), start=True, stop=True)\
                .then_inc(self.f_mean, 1)
        for c in range(4):
            e.wait_ge(self.f_sq, c + 1)
            e.matmul(self.var_bank(c)[:, :], g.mean_mat, g.sm[:, c, :], start=True, stop=True)\
                .then_inc(self.f_var, 1)

    def var_bank(self, c):
        g = self.g
        return (g.pS[0], g.pS[1], g.pT, g.pC)[c]

    def xs(self, c):
        return self.g.x[:, 2 * c:2 * c + 2, :].rearrange("p b l -> p (b l)")

    def act(self, e):
        g = self.g
        bank = g.pS

        def high_sources():
            for half in range(2):
                for m, src in enumerate((self.z, self.u)):
                    if half == 0:
                        e.wait_ge((self.z_loaded, self.u_loaded)[m], 16)
                    for b in (4 * half, 4 * half + 2):
                        e.activation(self.zu[m][0][:, b:b + 2, :], src[:, b:b + 2, :], ACT.Copy)\
                            .then_inc(self.src_hi, 1)

        def high_weights(k):
            ws = slice(4 * P * k, 4 * P * (k + 1))
            e.activation(g.wS[:, 0, ws], g.wA[:, ws], ACT.Copy).then_inc(self.w_hi, 1)

        def high_qk(p, groups=range(8)):
            for n in groups:
                q, half, chunk = self.QK[n]
                e.wait_ge(self.s_full, 24 * p + n + 1)
                src = bank[n % 2][:, :].rearrange("p (b l) -> p b l", b=4)
                bs, ls = slice(4 * half, 4 * half + 4), slice(chunk * P, chunk * P + P)
                if q == 0:
                    i = e.activation(self.q[0][:, bs, ls], src, ACT.Identity, bias=self.rwb)
                else:
                    for h in range(2):
                        rows = slice(64 * h, 64 * h + 64)
                        i = e.activation(self.kz[0][rows, bs, h, ls], src[rows], ACT.Copy,
                                         scale=self.SCALE)
                        if h == 0:
                            i.then_inc(self.qk_hi, 1)
                i.then_inc(self.qk_hi, 1)

        def exps(u, it, p):
            e.wait_ge(self.nmax, 16 * p + 2 * u + it + 1)
            e.wait_ge(self.s_full, 24 * p + 8 + 2 * u + it + 1)
            if not isinstance(p, int) or p > 0 or u >= 4:
                e.wait_ge(self.t_full, 16 * p + 2 * (u - 4) + 2)
                e.wait_ge((self.norm0, self.norm1)[it], 8 * p + u - 3)
            for h in range(2):
                i = e.activation(self.E[:, u % 4, it, h, :], bank[it][:, h * D:h * D + D], ACT.Exp,
                                 bias=self.st[:, 1, u % 4, it, h:h + 1],
                                 accum_out=self.st[:, 2, u % 4, it, h:h + 1])
            i.then_inc(self.s_free, 1)

        def evacuate_t(u, p):
            e.wait_ge(self.t_full, 16 * p + 2 * u + 2)
            e.activation(self.PT[:, u % 2, 1, :, :], g.pT[:, :].rearrange("p (h l) -> p h l", h=2),
                         ACT.Copy).then_inc(self.pt1, 1)

        def steps(slots, p, more):
            for s in slots:
                if s < B:
                    exps(s, 0, p)
                if 0 <= s - 2 < B:
                    evacuate_t(s - 2, p)
                if s < B:
                    exps(s, 1, p)
                if more and s in (4, 5):
                    if s == 4:
                        e.wait_ge(self.w_loaded, 16 * (p + 2))
                    high_weights(s - 4)

        def pair(p, more):
            for t in range(4):
                steps([B + t], p - 1, True)
                high_qk(p, [2 * t, 2 * t + 1])
            steps(range(B), p, more)

        e.wait_ge(self.w_loaded, 16)
        for k in range(2):
            high_weights(k)
        high_sources()
        high_qk(0)
        steps(range(B), 0, True)
        with e.Fori(1, NPAIR - 1) as p:
            pair(p, True)
        pair(NPAIR - 1, False)
        steps(range(B, B + 4), NPAIR - 1, False)
        for c in range(4):
            e.wait_ge(self.f_xc, c + 1)
            e.activation(g.sm[:, c, :], self.xs(c), ACT.Square).then_inc(self.f_sq, 1)
            if c >= 2:
                self.std(e, c - 2)
        self.std(e, 2)
        self.std(e, 3)

    def std(self, e, c):
        e.wait_ge(self.f_var, c + 1)
        e.activation(self.g.E[:, c, 0:512], self.var_bank(c)[:, :], ACT.Sqrt, bias=self.eps)\
            .then_inc(self.f_sd, 1)

    def dve(self, e):
        g = self.g
        bank = g.pS

        def maxes(u, it, p):
            e.wait_ge(self.s_full, 24 * p + 8 + 2 * u + it + 1)
            e.tensor_reduce(self.st[:, 1, u % 4, it, :],
                            bank[it][:, :].rearrange("p (h l) -> p h l", h=2), AX.X, ALU.max,
                            negate=True).then_inc(self.nmax, 1)

        def reciprocals(u, it, p):
            e.wait_ge(self.s_free, 16 * p + 2 * u + it + 1)
            e.reciprocal(self.st[:, 3, u % 4, it, :], self.st[:, 2, u % 4, it, :])\
                .then_inc(self.rec, 1)

        def normalise(u, p):
            e.wait_ge(self.rec, 16 * p + 2 * u + 2)
            for h in range(2):
                i = e.tensor_scalar(self.E[:, u % 4, 1, h, :], self.E[:, u % 4, 1, h, :],
                                    self.st[:, 3, u % 4, 1, h:h + 1], None, ALU.mult)
            i.then_inc(self.norm1, 1)

        def evacuate_t(u, p):
            e.wait_ge(self.t_full, 16 * p + 2 * u + 1)
            e.tensor_copy(self.PT[:, u % 2, 0, :, :], g.pT[:, :].rearrange("p (h l) -> p h l", h=2))\
                .then_inc(self.pt0, 1)

        def evacuate_c(u, p):
            e.wait_ge(self.c_full, 8 * p + u + 1)
            if not (isinstance(p, int) and p == 0 and u < 2):
                e.wait_ge(self.acc_done, 8 * p + u - 1)
            e.tensor_copy(g.cx[:, u % 2, :], g.pC[:, 0:D]).then_inc(self.ctx, 1)

        def evacuate_v(b, p):
            e.wait_ge(self.v_full, 8 * p + b + 1)
            e.tensor_copy(g.v[:, b, :], (g.pT, g.pC)[b % 2][:, 0:D]).then_inc(self.v_ready, 1)

        def steps(slots, p):
            for s in slots:
                if s < B:
                    maxes(s, 0, p)
                if 0 <= s - 2 < B:
                    evacuate_t(s - 2, p)
                if 0 <= s - 1 < B:
                    reciprocals(s - 1, 1, p)
                    normalise(s - 1, p)
                if s < 2:
                    evacuate_v(4 + 2 * s, p)
                if s < B:
                    reciprocals(s, 0, p)
                    maxes(s, 1, p)
                if s < 2:
                    evacuate_v(5 + 2 * s, p)
                if 0 <= s - 3 < B:
                    evacuate_c(s - 3, p)

        def low_qk(p, groups=range(8)):
            for n in groups:
                q, half, chunk = self.QK[n]
                high = 12 * p + (n if q == 0 else 4 + 2 * (n - 4))
                e.wait_ge(self.qk_hi, high + 1)
                src = bank[n % 2][:, :].rearrange("p (b l) -> p b l", b=4)
                bs, ls = slice(4 * half, 4 * half + 4), slice(chunk * P, chunk * P + P)
                if q == 0:
                    i = e.scalar_tensor_tensor(out=self.q[1][:, bs, ls], in0=src, scalar=self.rwb,
                                               in1=self.q[0][:, bs, ls].bitcast(F32),
                                               op0=ALU.add, op1=ALU.subtract)
                else:
                    for h in range(2):
                        rows = slice(64 * h, 64 * h + 64)
                        if h == 1:
                            e.wait_ge(self.qk_hi, high + 2)
                        i = e.scalar_tensor_tensor(out=self.kz[1][rows, bs, h, ls], in0=src[rows],
                                                   scalar=self.SCALE,
                                                   in1=self.kz[0][rows, bs, h, ls].bitcast(F32),
                                                   op0=ALU.mult, op1=ALU.subtract)
                i.then_inc(self.qk_lo, 1)

        def pair(p):
            for b in range(4):
                evacuate_v(b, p)
            steps(range(B), p)

        n = 0
        for half in range(2):
            for m, src in enumerate((self.z, self.u)):
                for b in (4 * half, 4 * half + 2):
                    e.wait_ge(self.src_hi, n + 1)
                    e.tensor_tensor(self.zu[m][1][:, b:b + 2, :], src[:, b:b + 2, :],
                                    self.zu[m][0][:, b:b + 2, :].bitcast(F32), ALU.subtract)\
                        .then_inc(self.src_lo, 1)
                    n += 1
                if half == 0:
                    evacuate_v(2 * m, 0)
                    evacuate_v(2 * m + 1, 0)
        low_qk(0)
        steps(range(B), 0)
        with e.Fori(1, NPAIR) as p:
            for t in range(4):
                steps([B + t], p - 1)
                low_qk(p, [2 * t, 2 * t + 1])
            pair(p)
        steps(range(B, B + 4), NPAIR - 1)
        for c in range(4):
            e.wait_ge(self.acc_done, 8 * (NPAIR - 1) + 2 * c + 2)
            e.scalar_tensor_tensor(out=self.xs(c), in0=g.acc[c][:, :], scalar=self.bo,
                                   in1=self.xs(c), op0=ALU.add, op1=ALU.add).then_inc(self.f_x, 1)
        for c in range(4):
            e.wait_ge(self.f_mean, c + 1)
            e.tensor_tensor(self.xs(c), self.xs(c), g.acc[c][:, :], ALU.subtract)\
                .then_inc(self.f_xc, 1)
        for c in range(4):
            e.wait_ge(self.f_sd, c + 1)
            e.reciprocal(g.PT[:, c % 2, 0:512], g.E[:, c, 0:512]).then_inc(self.f_rs, 1)
            e.wait_ge(self.f_rs, c + 1)
            e.wait_ge(self.f_sq, c + 1)
            e.tensor_tensor(self.xs(c), self.xs(c), g.PT[:, c % 2, 0:512], ALU.mult)\
                .then_inc(self.x_done, 2)
            if c >= 1:
                e.wait_ge(self.x_done, 2 * c)

    def pool(self, e):
        g = self.g
        def low_weights(k):
            ws = slice(2 * P * k, 2 * P * (k + 1))
            e.tensor_tensor(g.wS[:, 1, ws], g.wA[:, ws], g.wS[:, 0, ws].bitcast(F32), ALU.subtract)\
                .then_inc(self.w_lo, 1)

        def zeros(a, h):
            return a[64 - 64 * h:128 - 64 * h, :, h, :].bitcast(F32)

        for n, (dst, value) in enumerate(((self.eps, 1e-5), (g.eps[:, 1:2], -0.5),
                                          (zeros(self.kz[0], 0), 0.0), (zeros(self.kz[0], 1), 0.0))):
            if n:
                e.wait_ge(self.consts_set, n)
            e.memset(dst, value).then_inc(self.consts_set, 1)
        e.wait_ge(self.consts_set, 4)
        for k in range(4):
            e.wait_ge(self.w_hi, k // 2 + 1)
            low_weights(k)
        e.wait_ge(self.w_lo, 4)
        e.memset(zeros(self.kz[1], 0), 0.0).then_inc(self.consts_set, 1)
        e.wait_ge(self.consts_set, 5)
        e.memset(zeros(self.kz[1], 1), 0.0).then_inc(self.consts_set, 1)
        e.wait_ge(self.consts_set, 6)

        def pair(p, more):
            for u in range(B):
                e.wait_ge(self.rec, 16 * p + 2 * u + 1)
                e.tensor_tensor(self.E[:, u % 4, 0, :, :], self.E[:, u % 4, 0, :, :],
                                self.st[:, 3, u % 4, 0, :].unsqueeze(2).broadcast_to([P, 2, D]),
                                ALU.mult).then_inc(self.norm0, 1)
                if more and u >= 4:
                    e.wait_ge(self.w_hi, 2 * p + 3 + (u - 4) // 2)
                    low_weights(u - 4)

        pair(0, True)
        with e.Fori(1, NPAIR - 1) as p:
            pair(p, True)
        pair(NPAIR - 1, False)


GROUPS = B // 2


def row_stats(s, e, k):
    for b in (2 * k, 2 * k + 1):
        wait(e, s.x_ready[0], s.x_ready[1](b))
        e.bn_stats(s.bn[:, b, :], s.g.x[:, b, :]).then_inc(s.stats.sem, 1)
    for b in (2 * k, 2 * k + 1):
        wait(e, s.stats, b + 1)
        e.bn_aggr(s.mv[:, b, :], s.bn[:, b, :]).then_inc(s.aggr.sem, 1)


def row_rstd(s, e, k):
    two = slice(2 * k, 2 * k + 2)
    wait(e, s.aggr, 2 * k + 2)
    e.tensor_scalar(s.ve[:, two], s.mv[:, two, 1], s.eps, None, ALU.add).then_inc(s.veps.sem, 1)
    wait(e, s.veps, k + 1)
    e.tensor_tensor(s.rs[:, two], s.ve[:, two], s.g.eps[:, 1:2].broadcast_to([P, 2]), ALU.pow)\
        .then_inc(s.rstd.sem, 1)


class NormT:

    def __init__(self, g, name, dst, x_ready, prev, norm=None, split=False):
        self.g, self.dst, self.x_ready, self.prev, self.norm = g, dst, x_ready, prev, norm
        self.split = split
        if split:
            (self.hi, self.lo) = g.counts("norm_t_split", high_ready=B, low_ready=B)
        (self.stats, self.aggr, self.veps, self.rstd, self.h, self.t_full, self.done) = g.counts(
            "norm_t" if norm else "plain_t", stats_ready=B, mean_var_ready=B, var_eps_ready=GROUPS,
            rstd_ready=GROUPS, normalised_ready=B, transposed_in_bank=B, transposed_ready=B)
        self.bn = g.st[:, 64:112].rearrange("p (b k) -> p b k", b=B)
        self.mv = g.st[:, 112:128].rearrange("p (b k) -> p b k", b=B)
        self.ve = g.st[:, 128:136]
        self.rs = g.st[:, 136:144]
        self.eps = 1e-5
        self.banks = [g.pT, g.pC]

    def sp(self, e):
        pass

    def dve(self, e):
        if not self.norm:
            return
        for k in range(GROUPS + 1):
            if k < GROUPS:
                row_stats(self, e, k)
            if k >= 1:
                wait(e, self.rstd, k)
                for c in (2 * k - 2, 2 * k - 1):
                    if c >= 4:
                        wait(e, self.t_full, c - 3)
                    e.tensor_scalar(self.g.hn[:, c % 4, :], self.g.x[:, c, :], self.mv[:, c, 0:1],
                                    self.rs[:, c:c + 1], ALU.subtract, ALU.mult)\
                        .then_inc(self.h.sem, 1)

    def pool(self, e):
        if not self.norm:
            return
        for k in range(GROUPS):
            row_rstd(self, e, k)
            if self.split and k >= 2:
                self.low(e, k - 2)
        if self.split:
            self.low(e, GROUPS - 2)
            self.low(e, GROUPS - 1)

    def low(self, e, k):
        for b in (2 * k, 2 * k + 1):
            wait(e, self.hi, b + 1)
            hi, lo = (self.g.split[:, 1, part, :, b * P:b * P + P] for part in range(2))
            e.tensor_tensor(lo, self.dst[:, :, b * P:b * P + P], hi.bitcast(F32), ALU.subtract)\
                .then_inc(self.lo.sem, 1)

    def pe(self, e):
        g = self.g
        for sem, value in self.prev:
            wait(e, sem, value)
        for b in range(B):
            if self.norm:
                wait(e, self.h, b + 1)
            else:
                wait(e, self.x_ready[0], self.x_ready[1](b))
            if b >= 2:
                wait(e, self.done, b - 1)
            for c in range(KC):
                src = g.hn[:, b % 4, c * P:c * P + P] if self.norm else g.x[:, b, c * P:c * P + P]
                mm = e.transpose(self.banks[b % 2][:, c * P:c * P + P], src, g.ident)
            mm.then_inc(self.t_full.sem, 1)

    def act(self, e):
        g = self.g
        for b in range(B):
            wait(e, self.t_full, b + 1)
            bank = self.banks[b % 2]
            if self.norm:
                scale, offset = self.norm
                for c in range(KC):
                    i = e.activation(self.dst[:, c, b * P:b * P + P], bank[:, c * P:c * P + P],
                                     ACT.Identity, scale=scale[:, c:c + 1], bias=offset[:, c:c + 1])
            else:
                i = e.activation(self.dst[:, :, b * P:b * P + P],
                                 bank[:, 0:D].rearrange("p (c t) -> p c t", c=KC), ACT.Copy)
            i.then_inc(self.done.sem, 1)
            if self.split and b >= 1:
                self.high(e, b - 1)
        if self.split:
            self.high(e, B - 1)

    def high(self, e, b):
        wait(e, self.done, b + 1)
        ts = slice(b * P, b * P + P)
        e.activation(self.g.split[:, 1, 0, :, ts], self.dst[:, :, ts], ACT.Copy).then_inc(self.hi.sem, 1)

    def read_x(self):
        return (self.h, B) if self.norm else (self.t_full, B)

    def drained(self, batches=B):
        return [(self.done, batches)] + ([(self.lo, batches)] if self.split else [])


class SplitContext:

    def __init__(self, g, free):
        self.g, self.free = g, free
        self.hi, self.lo = g.sem("context_high_ready"), g.sem("context_low_ready")

    def sp(self, e):
        pass

    pe = pool = sp

    def act(self, e):
        g = self.g
        for sem, value in self.free:
            wait(e, sem, value)
        for c in range(KC):
            for half in range(2):
                ts = slice(half * HALF, half * HALF + HALF)
                e.activation(g.split[:, 0, 0, c, ts], g.cT[:, c, ts], ACT.Copy).then_inc(self.hi, 1)

    def dve(self, e):
        g = self.g
        for c in range(KC):
            for half in range(2):
                ts = slice(half * HALF, half * HALF + HALF)
                e.wait_ge(self.hi, 2 * c + half + 1)
                e.tensor_tensor(g.split[:, 0, 1, c, ts], g.cT[:, c, ts],
                                g.split[:, 0, 0, c, ts].bitcast(F32), ALU.subtract).then_inc(self.lo, 1)

    def drained(self):
        return [(self.lo, 4)]


class Project:

    def __init__(self, g, name, prev, w_loaded, q_src, kv_src, wq, wk, wv, bq, bk, bv, groups,
                 keys_ahead=False):
        self.g, self.prev, self.w_loaded, self.keys_ahead = g, prev, w_loaded, keys_ahead
        self.srcs, self.ws, self.bs = (kv_src, q_src), (wk, wq), (bk, bq)
        self.kv_src, self.wv, self.bv, self.groups = kv_src, wv, bv, groups
        (self.full, self.qk, self.vs, self.ones) = g.counts(
            "project", projection_in_bank=16, q_k_ready=8, v_ready=B, v_ones_set=2)
        self.qT = g.qT[:, :].rearrange("p (m t) -> p m t", m=2)
        self.kT = g.kT[:, 0:2 * T].rearrange("p (m t) -> p m t", m=2)
        self.vx = g.big[:, 4096:8192].rearrange("p (b g n) -> p b g n", b=B, g=4)
        self.banks = g.acc

    def sp(self, e):
        pass

    def project(self, e, which):
        n = 4 * which
        for half in range(2):
            if half == 1 and not (self.keys_ahead and which == 0):
                for sem, value in self.prev:
                    wait(e, sem, value)
            for m in range(2):
                if n >= 4:
                    wait(e, self.qk, n - 3)
                for c in range(KC):
                    mm = e.matmul(self.banks[n % 4][:, :], self.ws[which][:, c, m * P:m * P + P],
                                  self.srcs[which][:, c, half * HALF:half * HALF + HALF],
                                  start=c == 0, stop=c == KC - 1)
                mm.then_inc(self.full.sem, 1)
                n += 1

    def pe(self, e):
        for sem, value in self.half_prev + self.w_loaded:
            wait(e, sem, value)
        if not self.keys_ahead:
            self.project(e, 0)
        self.project(e, 1)
        width = self.wv.shape[2]
        for b in range(B):
            if b < 4:
                wait(e, self.qk, 5 + b)
            else:
                wait(e, self.vs, b - 3)
            for c in range(KC):
                mm = e.matmul(self.banks[b % 4][:, 0:width], self.kv_src[:, c, b * P:b * P + P],
                              self.wv[:, c, :], start=c == 0, stop=c == KC - 1)
            mm.then_inc(self.full.sem, 1)

    def evacuate(self, e, which):
        n, dst = 4 * which, (self.kT, self.qT)[which]
        for half in range(2):
            for m in range(2):
                wait(e, self.full, n + 1)
                e.activation(dst[:, m, half * HALF:half * HALF + HALF], self.banks[n % 4][:, :],
                             ACT.Identity, bias=self.bs[which][:, m:m + 1]).then_inc(self.qk.sem, 1)
                n += 1

    def act(self, e):
        if not self.keys_ahead:
            self.evacuate(e, 0)
        self.evacuate(e, 1)

    def dve(self, e):
        n = 64 * self.groups
        wait(e, self.ones, 2)
        for b in range(B):
            wait(e, self.full, 8 + b + 1)
            e.tensor_tensor(self.vx[:, b, 0:self.groups, 0:64],
                            self.banks[b % 4][:, 0:n].rearrange("p (g n) -> p g n", g=self.groups),
                            self.bv[:, 0:n].rearrange("p (g n) -> p g n", g=self.groups),
                            ALU.add).then_inc(self.vs.sem, 1)

    def pool(self, e):
        for sem, value in self.prev:
            wait(e, sem, value)
        e.memset(self.vx[:, :, 0:self.groups, 64:65], 1.0).then_inc(self.ones.sem, 1)
        wait(e, self.ones, 1)
        e.memset(self.vx[:, :, 0:self.groups, 65:128], 0.0).then_inc(self.ones.sem, 1)

    def drained(self):
        return [(self.qk, 8), (self.vs, B), (self.ones, 2)]


class SmallHeads:

    def __init__(self, g, name, project, hd, scale, multiply, masks_ready):
        self.g, self.hd, self.scale, self.multiply = g, hd, scale, multiply
        self.keys_ready = [(project.qk, 4)]
        self.q_ready = [(project.qk, 8)]
        self.v_ready = [(project.vs, B), (project.ones, 2)]
        self.masks_ready = masks_ready
        self.one_mask = False
        self.G = (8 if hd == 8 else 4)
        self.per_tile = self.G // 2
        self.heads = g.head8 if hd == 8 else g.head16
        self.N = B * self.G
        (self.keys, self.s_full, self.scaled, self.masked, self.min, self.exp,
         self.t_full, self.pt, self.c_full, self.rec, self.done) = g.counts(
            "small_heads", keys_masked=self.N, scores_in_bank=self.N,
            scores_scaled=self.N, scores_masked=self.N if multiply else 0, min_ready=self.N,
            exp_ready=self.N, transposed_in_bank=self.N, probsT_ready=self.N,
            context_in_bank=self.N, recip_ready=self.N, context_ready=self.N)
        if not multiply:
            self.masked = self.scaled
        self.qT = g.qT[:, :].rearrange("p (m t) -> p m t", m=2)
        self.kT = g.kT[:, 0:2 * T].rearrange("p (m t) -> p m t", m=2)
        self.vx = g.big[:, 4096:8192].rearrange("p (b g n) -> p b g n", b=B, g=4)
        self.km = g.km[:, :, :].rearrange("p n (j t) -> p n j t", j=4)
        self.sm = g.sm[:, :, :].rearrange("p n (j t) -> p n j t", j=4)
        self.E = g.E[:, :, 0:512].rearrange("p n (j t) -> p n j t", j=4)
        self.PT = g.PT[:, :, 0:512].rearrange("p n (j t) -> p n j t", j=4)
        self.mn = g.st[:, 160:176].rearrange("p (n j) -> p n j", n=4)
        self.rc = g.st[:, 176:192].rearrange("p (n j) -> p n j", n=4)
        self.bS = g.pS
        self.bT = [g.pT, g.acc[0]]
        self.bC = [g.pC, g.acc[1]]

    def sp(self, e):
        pass

    def unit(self, n):
        b, gr = divmod(n, self.G)
        return b, gr, gr // self.per_tile, 4 * (gr % self.per_tile)

    def pool(self, e):
        for sem, value in self.keys_ready:
            wait(e, sem, value)
        for n in range(self.N + 2):
            if n == 2:
                for sem, value in self.masks_ready:
                    wait(e, sem, value)
            if n < self.N:
                b, _, m, h = self.unit(n)
                if n >= 3:
                    wait(e, self.s_full, n - 2)
                e.tensor_tensor(self.km[:, n % 3], self.kT[:, m, b * P:b * P + P].unsqueeze(1)
                                .broadcast_to([P, 4, P]),
                                self.heads[:, h:h + 4].unsqueeze(2).broadcast_to([P, 4, P]),
                                ALU.mult).then_inc(self.keys.sem, 1)
            if self.multiply and n >= 2:
                k = n - 2
                b = self.unit(k)[0]
                wait(e, self.scaled, k + 1)
                e.tensor_tensor(self.sm[:, k % 4], self.sm[:, k % 4], self.amask(b), ALU.subtract)\
                    .then_inc(self.masked.sem, 1)

    def mul_mask(self, b):
        b = 0 if self.one_mask else b
        return self.g.mask[:, b, :].unsqueeze(1).broadcast_to([P, 4, P])

    def amask(self, b):
        b = 0 if self.one_mask else b
        return self.g.amask[:, b, :].unsqueeze(1).broadcast_to([P, 4, P])

    def pe(self, e):
        g = self.g
        for sem, value in self.q_ready:
            wait(e, sem, value)
        for s in range(self.N + 4):
            if s < self.N:
                n = s
                b, _, m, _ = self.unit(n)
                wait(e, self.keys, n + 1)
                if n >= 2:
                    wait(e, self.scaled, n - 1)
                e.matmul(self.bS[n % 2][:, :], self.qT[:, m, b * P:b * P + P], self.km[:, n % 3],
                         start=True, stop=True).then_inc(self.s_full.sem, 1)
            n = s - 3
            if 0 <= n < self.N:
                wait(e, self.exp, n + 1)
                if n >= 2:
                    wait(e, self.pt, n - 1)
                for j in range(4):
                    mm = e.transpose(self.bT[n % 2][:, j * P:j * P + P], self.E[:, n % 4, j, :],
                                     g.ident)
                mm.then_inc(self.t_full.sem, 1)
            n = s - 4
            if 0 <= n < self.N:
                b, gr, _, _ = self.unit(n)
                if n == 0:
                    for sem, value in self.v_ready:
                        wait(e, sem, value)
                wait(e, self.pt, n + 1)
                if n >= 2:
                    wait(e, self.done, n - 1)
                for j in range(4):
                    mm = e.matmul(self.bC[n % 2][:, j * P:j * P + P], self.PT[:, n % 2, j, :],
                                  self.vx[:, b, 0 if self.hd == 8 else gr, :], start=True, stop=True)
                mm.then_inc(self.c_full.sem, 1)

    def act(self, e):
        for s in range(self.N + 2):
            n = s - 2
            if n >= 0:
                wait(e, self.t_full, n + 1)
                e.activation(self.PT[:, n % 2], self.bT[n % 2][:, :]
                             .rearrange("p (j t) -> p j t", j=4), ACT.Copy).then_inc(self.pt.sem, 1)
            n = s
            if n < self.N:
                wait(e, self.min, n + 1)
                if n >= 4:
                    wait(e, self.t_full, n - 3)
                for j in range(4):
                    i = e.activation(self.E[:, n % 4, j, :], self.sm[:, n % 4, j, :], ACT.Exp,
                                     bias=self.mn[:, n % 4, j:j + 1], scale=-1.0)
                i.then_inc(self.exp.sem, 1)

    def dve(self, e):
        g, hd = self.g, self.hd
        for sem, value in self.masks_ready:
            wait(e, sem, value)
        for s in range(self.N + 5):
            n = s
            if n < self.N:
                b = self.unit(n)[0]
                wait(e, self.s_full, n + 1)
                if n >= 4:
                    wait(e, self.exp, n - 3)
                e.scalar_tensor_tensor(out=self.sm[:, n % 4],
                                       in0=self.bS[n % 2][:, :].rearrange("p (j t) -> p j t", j=4),
                                       scalar=-self.scale, in1=self.mul_mask(b), op0=ALU.mult,
                                       op1=ALU.mult if self.multiply else ALU.subtract)\
                    .then_inc(self.scaled.sem, 1)
            n = s - 1
            if 0 <= n < self.N:
                wait(e, self.masked, n + 1)
                e.tensor_reduce(self.mn[:, n % 4, :], self.sm[:, n % 4], AX.X, ALU.min)\
                    .then_inc(self.min.sem, 1)
            n = s - 5
            if n >= 0:
                b, gr, _, _ = self.unit(n)
                bank = self.bC[n % 2]
                wait(e, self.c_full, n + 1)
                e.reciprocal(self.rc[:, n % 4, :],
                             bank[:, :].rearrange("p (j c) -> p j c", j=4)[:, :, 64])\
                    .then_inc(self.rec.sem, 1)
                wait(e, self.rec, n + 1)
                step, first = (P, hd * gr) if hd == 8 else (P + hd, 0)
                src = bass.AP(tensor=bank, offset=first, ap=[[512, P], [step, 4], [1, hd]])
                e.tensor_tensor(g.v[:, b, 4 * hd * gr:4 * hd * (gr + 1)]
                                .rearrange("p (j d) -> p j d", j=4), src,
                                self.rc[:, n % 4, :].unsqueeze(2).broadcast_to([P, 4, hd]),
                                ALU.mult).then_inc(self.done.sem, 1)

    def drained(self):
        return [(self.done, self.N), (self.pt, self.N)]


class OutProject:

    def __init__(self, g, name, prev, heads, wo, bo, x_read, w_loaded):
        self.g, self.prev, self.heads, self.wo, self.bo = g, prev, heads, wo, bo
        self.x_read, self.w_loaded = x_read, w_loaded
        (self.xb, self.t_full, self.cx, self.o_full, self.x) = g.counts(
            "out_project", x_plus_bias_ready=B, transposed_in_bank=B, contextT_ready=B,
            output_in_bank=B, x_ready=B)
        self.bT = [g.acc[2], g.acc[3]]
        self.bO = [g.pS[0], g.pS[1]]

    def sp(self, e):
        pass

    def pool(self, e):
        pass

    def add_bias(self, e):
        wait(e, *self.x_read)
        for b in range(B):
            e.tensor_tensor(self.g.x[:, b, :], self.g.x[:, b, :], self.bo, ALU.add)\
                .then_inc(self.xb.sem, 1)

    def pe(self, e):
        g = self.g
        for sem, value in self.prev + self.w_loaded:
            wait(e, sem, value)
        for s in range(B + 1):
            if s < B:
                b = s
                if b >= 2:
                    wait(e, self.cx, b - 1)
                for c in range(KC):
                    mm = e.transpose(self.bT[b % 2][:, c * P:c * P + P], g.v[:, b, c * P:c * P + P],
                                     g.ident)
                mm.then_inc(self.t_full.sem, 1)
            b = s - 1
            if b >= 0:
                wait(e, self.cx, b + 1)
                if b >= 2:
                    wait(e, self.x, b - 1)
                for c in range(KC):
                    mm = e.matmul(self.bO[b % 2][:, 0:D], g.cx[:, b % 2, c * P:c * P + P],
                                  self.wo[:, c, :], start=c == 0, stop=c == KC - 1)
                mm.then_inc(self.o_full.sem, 1)

    def act(self, e):
        g = self.g
        for b in range(B):
            wait(e, self.t_full, b + 1)
            if b >= 2:
                wait(e, self.o_full, b - 1)
            e.activation(g.cx[:, b % 2, :], self.bT[b % 2][:, 0:D], ACT.Copy).then_inc(self.cx.sem, 1)

    def dve(self, e):
        g = self.g
        for b in range(B):
            wait(e, self.xb, b + 1)
            wait(e, self.o_full, b + 1)
            e.tensor_tensor(g.x[:, b, :], self.bO[b % 2][:, 0:D], g.x[:, b, :], ALU.add)\
                .then_inc(self.x.sem, 1)

    def drained(self):
        return [(self.x, B), (self.cx, B)]


class NormRows:

    def __init__(self, g, name, x_ready, eps, gamma, beta):
        self.g, self.x_ready, self.eps, self.gamma, self.beta = g, x_ready, eps, gamma, beta
        (self.stats, self.aggr, self.veps, self.rstd, self.scaled, self.x) = g.counts(
            "norm_rows", stats_ready=B, mean_var_ready=B, var_eps_ready=GROUPS, rstd_ready=GROUPS,
            scaled_ready=B, x_ready=B)
        self.bn = g.st[:, 64:112].rearrange("p (b k) -> p b k", b=B)
        self.mv = g.st[:, 112:128].rearrange("p (b k) -> p b k", b=B)
        self.ve = g.st[:, 128:136]
        self.rs = g.st[:, 136:144]

    def sp(self, e):
        pass

    pe = act = sp

    def dve(self, e):
        g = self.g
        for k in range(GROUPS + 1):
            if k < GROUPS:
                row_stats(self, e, k)
                for b in (2 * k, 2 * k + 1):
                    wait(e, self.aggr, b + 1)
                    e.scalar_tensor_tensor(out=g.x[:, b, :], in0=g.x[:, b, :],
                                           scalar=self.mv[:, b, 0:1], in1=self.gamma,
                                           op0=ALU.subtract, op1=ALU.mult).then_inc(self.scaled.sem, 1)
            if k >= 1:
                wait(e, self.rstd, k)
                for b in (2 * k - 2, 2 * k - 1):
                    wait(e, self.scaled, b + 1)
                    e.scalar_tensor_tensor(out=g.x[:, b, :], in0=g.x[:, b, :],
                                           scalar=self.rs[:, b:b + 1], in1=self.beta,
                                           op0=ALU.mult, op1=ALU.add).then_inc(self.x.sem, 1)

    def pool(self, e):
        for k in range(GROUPS):
            row_rstd(self, e, k)


class Mlp:

    def __init__(self, g, name, prev, func, b1, b2, x_read, ins_names, w_free):
        self.g, self.prev, self.func, self.b1, self.b2, self.x_read = g, prev, func, b1, b2, x_read
        self.ins_names, self.w_free = ins_names, w_free
        (self.w_loaded, self.xb, self.f_full, self.gelu, self.o_full, self.x) = g.counts(
            "mlp", weights_loaded=32, x_plus_bias_ready=B, hidden_in_bank=16,
            gelu_ready=16, output_in_bank=B, x_ready=B)
        self.gT = g.big[:, :].rearrange("p (f t) -> p f t", f=8)
        self.bO = [g.pS[0], g.pS[1], g.pT, g.pC]

    def sp(self, e):
        pass

    def load(self, e):
        g = self.g
        for sem, value in self.w_free:
            wait(e, sem, value)
        e.dma_start(g.w1[:, :, :], g.ins[self.ins_names[0]]).then_inc(self.w_loaded.sem, 16)
        e.dma_start(g.w2[:, :, :], g.ins[self.ins_names[1]]).then_inc(self.w_loaded.sem, 16)

    def pool(self, e):
        wait(e, *self.x_read)
        for b in range(B):
            e.tensor_tensor(self.g.x[:, b, :], self.g.x[:, b, :], self.b2, ALU.add)\
                .then_inc(self.xb.sem, 1)

    def pe(self, e):
        g = self.g
        wait(e, self.w_loaded, 32)
        n = 0
        for half in range(2):
            for sem, value in (self.half_prev, self.prev)[half]:
                wait(e, sem, value)
            for f in range(8):
                if n >= 4:
                    wait(e, self.gelu, n - 3)
                for c in range(KC):
                    mm = e.matmul(g.acc[n % 4][:, :], g.w1[:, c, f * P:f * P + P],
                                  g.hT[:, c, half * HALF:half * HALF + HALF],
                                  start=c == 0, stop=c == KC - 1)
                mm.then_inc(self.f_full.sem, 1)
                n += 1
        for b in range(B):
            wait(e, self.gelu, 8 if b < 4 else 16)
            if b >= 4:
                wait(e, self.x, b - 3)
            for f in range(8):
                mm = e.matmul(self.bO[b % 4][:, 0:D], self.gT[:, f, b * P:b * P + P], g.w2[:, f, :],
                              start=f == 0, stop=f == 7)
            mm.then_inc(self.o_full.sem, 1)

    def act(self, e):
        n = 0
        for half in range(2):
            for f in range(8):
                wait(e, self.f_full, n + 1)
                e.activation(self.gT[:, f, half * HALF:half * HALF + HALF], self.g.acc[n % 4][:, :],
                             self.func, bias=self.b1[:, f:f + 1]).then_inc(self.gelu.sem, 1)
                n += 1

    def dve(self, e):
        g = self.g
        for b in range(B):
            wait(e, self.xb, b + 1)
            wait(e, self.o_full, b + 1)
            e.tensor_tensor(g.x[:, b, :], self.bO[b % 4][:, 0:D], g.x[:, b, :], ALU.add)\
                .then_inc(self.x.sem, 1)

    def drained(self):
        return [(self.x, B), (self.gelu, 16)]


class CrossAttention:

    SCALE = 128 ** -0.5
    PACK = 3 * KC * D + 6

    def __init__(self, g, name, layer, prev, x_read, bo, w_free, wo_free):
        self.g, self.layer, self.prev, self.x_read, self.bo = g, layer, prev, x_read, bo
        self.w_free, self.wo_free = w_free, wo_free
        (self.w_loaded, self.bv_loaded, self.wo_loaded, self.bvx, self.bk, self.xb,
         self.s_full, self.s_free, self.v_full, self.v_ready, self.t_full, self.pt, self.c_full,
         self.ctx, self.acc_done, self.q_bias, self.nmax, self.rec, self.norm, self.x,
         self.w_hi, self.w_lo) = g.counts(
            "cross", pair_weights_loaded=16 * NPAIR, value_rows_loaded=16 * NPAIR,
            wo_loaded=16 * NPAIR, value_bias_ready=NPAIR, learnt_key_ready=2 * NPAIR,
            x_plus_bias_ready=B, s_bank_full=16 * NPAIR, s_bank_free_by_act=16 * NPAIR, values_in_bank=8 * NPAIR,
            values_ready=8 * NPAIR, t_bank_full=8 * NPAIR, probsT_ready=8 * NPAIR,
            c_bank_full=8 * NPAIR, ctx_ready=8 * NPAIR, acc_units_done=8 * NPAIR,
            scaled_q_bias_ready=NPAIR, negmax_ready=8 * NPAIR, recip_ready=8 * NPAIR,
            probs_normalised=8 * NPAIR, x_ready=B, weights_high_ready=2 * NPAIR,
            weights_low_ready=2 * NPAIR)
        self.w = g.wS[:, :, :].rearrange("p k (q c n) -> p k q c n", q=3, c=KC)
        self.bias = g.wA[:, 3 * KC * D:self.PACK]
        self.wo = g.wB[:, 0:2 * D].rearrange("p (h n) -> p h n", h=2)
        self.bias_v = g.wB[:, 2 * D:2 * D + 2]
        self.qT = g.qT[:, :].rearrange("p (h t) -> p h t", h=2)
        self.kT = g.kT[:, :].rearrange("p (h b t) -> p h b t", h=2, b=B)
        self.E = g.E[:, :, 0:2 * (P + 1)].rearrange("p n (h t) -> p n h t", h=2)
        self.PT = g.PT[:, :, 0:D].rearrange("p n (h t) -> p n h t", h=2)
        self.st = g.st[:, 192:224].rearrange("p (k n h) -> p k n h", k=4, n=4)
        self.qb = g.st[:, 224:226]
        self.ring = Ring(["act"] * 16, 2)

    def sp(self, e):
        at = Layer0.at
        w, rows, wo = self.sources()
        with e.Fori(1, NPAIR) as p:
            wait(e, self.v_ready, 8 * p)
            self.load_w(e, at(w, p), rows[bass.ds(p, 1)])
            wait(e, self.acc_done, 8 * p)
            self.load_wo(e, at(wo, p))

    def sources(self):
        return (self.g.ins[f"{k}{self.layer}"] for k in ("l2_w_", "l2_bv_", "l2_wo_"))

    def load_first(self, e):
        w, rows, wo = self.sources()
        for sem, value in self.w_free:
            wait(e, sem, value)
        self.load_w(e, w[0:1].rearrange("a p n -> (a p) n"), rows[0:1])
        for sem, value in self.wo_free:
            wait(e, sem, value)
        self.load_wo(e, wo[0:1].rearrange("a p n -> (a p) n"))

    def load_w(self, e, w, rows):
        g = self.g
        e.dma_start(g.wA[:, 0:self.PACK], w).then_inc(self.w_loaded.sem, 16)
        e.dma_start(g.bv[:, :, :].rearrange("p k n -> p (k n)"), rows.broadcast_to([P, 2 * D]))\
            .then_inc(self.bv_loaded.sem, 16)

    def project(self, e, which, p=0):
        g = self.g
        if which == 0:
            wait(e, self.w_lo, 2 * p + 1)
        n = 4 * which
        for half in range(2):
            if which == 1 and isinstance(p, int) and p == 0:
                for sem, value in (self.half_prev, self.prev)[half]:
                    wait(e, sem, value)
            for h in range(2):
                self.claim(e, n, p)
                for i, (c, kw, ks) in enumerate(PARTS):
                    mm = e.matmul(g.pS[n % 2][:, :], self.w[:, kw, 1 - which, c, h * P:h * P + P],
                                  g.split[:, which, ks, c, half * HALF:half * HALF + HALF],
                                  start=i == 0, stop=i == len(PARTS) - 1)
                mm.then_inc(self.s_full.sem, 1)
                n += 1

    def claim(self, e, n, p):
        need = self.ring.before(n, p)
        if need is not None:
            wait(e, self.s_free, need[1])

    def evacuate(self, e, which, p=0):
        n = 4 * which
        for half in range(2):
            for h in range(2):
                wait(e, self.s_full, 16 * p + n + 1)
                bank = self.g.pS[n % 2]
                if which == 0:
                    i = e.activation(self.kT[:, h, 4 * half:4 * half + 4, 0:P],
                                     bank[:, :].rearrange("p (b t) -> p b t", b=4),
                                     ACT.Identity, bias=self.bias[:, 2 + h:3 + h])
                else:
                    if n == 4:
                        wait(e, self.q_bias, p + 1)
                    i = e.activation(self.qT[:, h, half * HALF:half * HALF + HALF], bank[:, :],
                                     ACT.Identity, bias=self.qb[:, h:h + 1], scale=self.SCALE)
                i.then_inc(self.s_free.sem, 1)
                n += 1

    def load_wo(self, e, wo):
        e.dma_start(self.g.wB[:, :], wo).then_inc(self.wo_loaded.sem, 16)

    def pe(self, e):
        g = self.g
        bank = g.pS

        def project_v(b, p):
            if b >= 2:
                wait(e, self.v_ready, 8 * p + b - 1)
            elif not (isinstance(p, int) and p == 0):
                wait(e, (self.pt, self.ctx)[b], 8 * p)
            if b == 0:
                wait(e, self.w_lo, 2 * p + 2)
            for i, (c, kw, ks) in enumerate(PARTS):
                mm = e.matmul((g.pT, g.pC)[b % 2][:, 0:D], g.split[:, 0, ks, c, b * P:b * P + P],
                              self.w[:, kw, 2, c, :], start=i == 0, stop=i == len(PARTS) - 1)
            mm.then_inc(self.v_full.sem, 1)

        def scores(u, p):
            self.claim(e, 8 + u, p)
            if u == 0:
                wait(e, self.s_free, 16 * p + 8)
                wait(e, self.bk, 2 * p + 2)
            for h in range(2):
                mm = e.matmul(bank[u % 2][:, h * (P + 1):(h + 1) * (P + 1)],
                              self.qT[:, h, u * P:u * P + P], self.kT[:, h, u, :],
                              start=True, stop=True)
            mm.then_inc(self.s_full.sem, 1)

        def transposes(u, p):
            wait(e, self.norm, 8 * p + u + 1)
            if u == 0:
                wait(e, self.v_ready, 8 * p + 7)
            if not (isinstance(p, int) and p == 0 and u == 0):
                wait(e, self.pt, 8 * p + u)
            for h in range(2):
                mm = e.transpose(g.pT[:, h * P:h * P + P], self.E[:, u % 4, h, 0:P], g.ident)
            mm.then_inc(self.t_full.sem, 1)

        def context(u, p):
            wait(e, self.pt, 8 * p + u + 1)
            if u == 0:
                wait(e, self.v_ready, 8 * p + 8)
            if not (isinstance(p, int) and p == 0 and u == 0):
                wait(e, self.ctx, 8 * p + u)
            for h in range(2):
                mm = e.matmul(g.pC[:, h * P:h * P + P], g.v[:, u, h * P:h * P + P],
                              self.PT[:, u % 2, h, :], start=True, stop=True)
            mm.then_inc(self.c_full.sem, 1)

        def output(u, p, first):
            wait(e, self.ctx, 8 * p + u + 1)
            if u == 0:
                wait(e, self.wo_loaded, 16 * (p + 1))
            for h in range(2):
                mm = e.matmul(g.acc[u // 2][:, (u % 2) * D:(u % 2) * D + D],
                              g.cx[:, u % 2, h * P:h * P + P], self.wo[:, h, :],
                              start=first and h == 0 and u % 2 == 0, stop=True,
                              skip_group_check=True)
            mm.then_inc(self.acc_done.sem, 1)

        def steps(slots, p, first):
            for s in slots:
                if s < B:
                    scores(s, p)
                if s < 3:
                    project_v(2 + 2 * s, p)
                    project_v(3 + 2 * s, p)
                if 0 <= s - 2 < B:
                    transposes(s - 2, p)
                if 0 <= s - 3 < B:
                    context(s - 3, p)
                if 0 <= s - 4 < B:
                    output(s - 4, p, first)

        self.project(e, 1)
        for b in range(2):
            project_v(b, 0)
        steps(range(B), 0, True)

        def pair(p, first):
            steps(range(B, B + 1), p - 1, first)
            self.project(e, 0, p)
            self.project(e, 1, p)
            steps(range(B + 1, B + 4), p - 1, first)
            for b in range(2):
                project_v(b, p)
            steps(range(B), p, False)

        pair(1, True)
        with e.Fori(2, NPAIR) as p:
            pair(p, False)
        steps(range(B, B + 4), NPAIR - 1, False)

    def act(self, e):
        g = self.g
        bank = g.pS

        def exps(u, p):
            wait(e, self.nmax, 8 * p + u + 1)
            if not isinstance(p, int) or p > 0 or u >= 4:
                wait(e, self.t_full, 8 * p + u - 3)
                wait(e, self.norm, 8 * p + u - 3)
            for h in range(2):
                i = e.activation(self.E[:, u % 4, h, :], bank[u % 2][:, h * (P + 1):(h + 1) * (P + 1)],
                                 ACT.Exp, bias=self.st[:, 1, u % 4, h:h + 1],
                                 accum_out=self.st[:, 2, u % 4, h:h + 1])
            i.then_inc(self.s_free.sem, 1)

        def evacuate_t(u, p):
            wait(e, self.t_full, 8 * p + u + 1)
            e.activation(self.PT[:, u % 2], g.pT[:, 0:D].rearrange("p (h t) -> p h t", h=2),
                         ACT.Copy).then_inc(self.pt.sem, 1)

        def steps(slots, p):
            for s in slots:
                if 0 <= s - 2 < B:
                    evacuate_t(s - 2, p)
                if s < B:
                    exps(s, p)

        self.evacuate(e, 1)
        steps(range(B), 0)
        with e.Fori(1, NPAIR) as p:
            steps(range(B, B + 1), p - 1)
            self.evacuate(e, 0, p)
            self.evacuate(e, 1, p)
            steps(range(B + 1, B + 4), p - 1)
            steps(range(B), p)
        steps(range(B, B + 4), NPAIR - 1)

    def dve(self, e):
        g = self.g
        bank = g.pS
        bias_v = self.bias_v.unsqueeze(2).broadcast_to([P, 2, P])

        def evacuate_v(b, p):
            if b == 0:
                wait(e, self.bvx, p + 1)
                wait(e, self.bk, 2 * p + 2)
            wait(e, self.v_full, 8 * p + b + 1)
            e.tensor_tensor(g.v[:, b, :], (g.pT, g.pC)[b % 2][:, 0:D], g.bv[:, 0, :], ALU.add)\
                .then_inc(self.v_ready.sem, 1)

        def maxes(u, p):
            wait(e, self.s_full, 16 * p + 8 + u + 1)
            e.tensor_reduce(self.st[:, 1, u % 4, :], bank[u % 2][:, 0:2 * (P + 1)]
                            .rearrange("p (h t) -> p h t", h=2), AX.X, ALU.max, negate=True)\
                .then_inc(self.nmax.sem, 1)

        def normalise(u, p):
            wait(e, self.s_free, 16 * p + 8 + u + 1)
            e.reciprocal(self.st[:, 3, u % 4, :], self.st[:, 2, u % 4, :]).then_inc(self.rec.sem, 1)
            wait(e, self.rec, 8 * p + u + 1)
            e.tensor_tensor(self.E[:, u % 4, :, 0:P], self.E[:, u % 4, :, 0:P],
                            self.st[:, 3, u % 4, :].unsqueeze(2).broadcast_to([P, 2, P]),
                            ALU.mult).then_inc(self.norm.sem, 1)

        def evacuate_c(u, p):
            wait(e, self.c_full, 8 * p + u + 1)
            if u == 0:
                wait(e, self.wo_loaded, 16 * (p + 1))
            if not (isinstance(p, int) and p == 0 and u < 2):
                wait(e, self.acc_done, 8 * p + u - 1)
            e.tensor_tensor(g.cx[:, u % 2, :].rearrange("p (h t) -> p h t", h=2),
                            g.pC[:, 0:D].rearrange("p (h t) -> p h t", h=2), bias_v, ALU.add)\
                .then_inc(self.ctx.sem, 1)

        def steps(slots, p, more):
            for s in slots:
                if s < B:
                    maxes(s, p)
                if s < 3:
                    evacuate_v(2 + 2 * s, p)
                if 0 <= s - 1 < B:
                    normalise(s - 1, p)
                if s < 3:
                    evacuate_v(3 + 2 * s, p)
                if 0 <= s - 3 < B:
                    evacuate_c(s - 3, p)
                if more and s == 5:
                    wait(e, self.w_loaded, 16 * (p + 2))
                    self.high(e, 0, 2 * KC * D)
                if more and s == 6:
                    self.high(e, 2 * KC * D, 3 * KC * D)

        def pair(p, more):
            for b in range(2):
                evacuate_v(b, p)
            steps(range(B), p, more)

        pair(0, True)
        with e.Fori(1, NPAIR - 1) as p:
            steps(range(B, B + 4), p - 1, True)
            pair(p, True)
        steps(range(B, B + 4), NPAIR - 2, True)
        pair(NPAIR - 1, False)
        steps(range(B, B + 4), NPAIR - 1, False)
        for b in range(B):
            wait(e, self.xb, b + 1)
            wait(e, self.acc_done, 8 * (NPAIR - 1) + 2 * (b // 2) + 2)
            e.tensor_tensor(g.x[:, b, :], g.acc[b // 2][:, (b % 2) * D:(b % 2) * D + D],
                            g.x[:, b, :], ALU.add).then_inc(self.x.sem, 1)

    def pool(self, e):
        g = self.g

        for sem, value in self.prev:
            wait(e, sem, value)
        self.learnt_keys(e)
        wait(e, *self.x_read)
        for b in range(B):
            e.tensor_tensor(g.x[:, b, :], g.x[:, b, :], self.bo, ALU.add).then_inc(self.xb.sem, 1)
        with e.Fori(1, NPAIR) as p:
            self.prepare(e, p)
            self.learnt_keys(e)

    def high(self, e, start, end):
        e.tensor_copy(self.g.wS[:, 0, start:end], self.g.wA[:, start:end]).then_inc(self.w_hi.sem, 1)

    def prepare(self, e, p):
        g = self.g
        wait(e, self.w_loaded, 16 * (p + 1))
        wait(e, self.bv_loaded, 16 * (p + 1))
        e.tensor_tensor(g.bv[:, 0, :], g.bv[:, 0, :], g.bv[:, 1, :], ALU.subtract)\
            .then_inc(self.bvx.sem, 1)
        e.tensor_scalar(self.qb, self.bias[:, 0:2], self.SCALE, None, ALU.mult)\
            .then_inc(self.q_bias.sem, 1)
        n, qk = 3 * KC * D, 2 * KC * D
        if isinstance(p, int) and p == 0:
            self.high(e, 0, qk)
            self.high(e, qk, n)
        wait(e, self.w_hi, 2 * p + 1)
        e.tensor_tensor(g.wS[:, 1, 0:qk], g.wA[:, 0:qk], g.wS[:, 0, 0:qk].bitcast(F32),
                        ALU.subtract).then_inc(self.w_lo.sem, 1)
        if not (isinstance(p, int) and p == 0):
            wait(e, self.s_full, 16 * p)
        wait(e, self.w_hi, 2 * p + 2)
        e.tensor_tensor(g.wS[:, 1, qk:n], g.wA[:, qk:n], g.wS[:, 0, qk:n].bitcast(F32),
                        ALU.subtract).then_inc(self.w_lo.sem, 1)

    def learnt_keys(self, e):
        for h in range(2):
            e.tensor_copy(self.kT[:, h, :, P], self.bias[:, 4 + h:5 + h].broadcast_to([P, B]))\
                .then_inc(self.bk.sem, 1)

    def drained(self):
        return [(self.x, B)]


def store(g, e, ready, base):
    done = g.sem("stored")
    for b in range(B):
        wait(e, ready, base[b])
        e.dma_start(g.out[b], g.x[:, b, :]).then_inc(done, 16)
    e.wait_ge(done, 16 * B)


def build_program(nc, ins, out, stop=None):
    with ExitStack() as ctx:
        g = Shared(nc, ctx, ins)
        g.out = out
        stages, last = plan(g, stop)
        block = ctx.enter_context(nc.Block())

        @block.sync
        def _(e):
            for s in stages:
                s.sp(e)
            store(g, e, *last)

        @block.tensor
        def _(e):
            for s in stages:
                s.pe(e)

        @block.scalar
        def _(e):
            for s in stages:
                s.act(e)

        @block.vector
        def _(e):
            for s in stages:
                s.dve(e)

        @block.gpsimd
        def _(e):
            for s in stages:
                s.pool(e)


class Loads:

    def __init__(self, g, name, loads, free=()):
        self.g, self.loads, self.free = g, loads, free
        self.sem = g.sem(f"{name}_loaded")

    def sp(self, e):
        for sem, value in self.free:
            wait(e, sem, value)
        for dst, src in self.loads:
            e.dma_start(dst, src).then_inc(self.sem, 16)

    def pe(self, e):
        pass

    act = dve = pool = pe

    def done(self):
        return [(self.sem, 16 * len(self.loads))]


class AdditiveMask:

    def __init__(self, g, name, loaded, free):
        self.g, self.loaded, self.free = g, loaded, free
        self.sem = g.sem(f"{name}_amask_ready")

    def pool(self, e):
        for sem, value in self.loaded + self.free:
            wait(e, sem, value)
        e.tensor_scalar(self.g.amask[:, :, :], self.g.mask[:, :, :], -1.0, 10000.0, ALU.add, ALU.mult)\
            .then_inc(self.sem, 1)

    def pe(self, e):
        pass

    act = dve = sp = pe

    def done(self):
        return [(self.sem, 1)]


def plan(g, stop):
    ins, col, row = g.ins, g.col, g.row
    by_batch = lambda sem: (sem, lambda b: b + 1)

    w1 = g.w1[:, :, :].rearrange("p c n -> p (c n)")
    l1_loads = Loads(g, "l1", [(w1[:, 0:1792], ins["l1_w"]), (g.mask[:, :, :], ins["mask0"])])
    l0 = Layer0(g)
    stages = [InputLoads(l0), l1_loads, l0]
    x_l0 = (l0.x_done, lambda b: 2 * (b // 2) + 2)
    l0_end = [(l0.f_sd, 4)]
    if stop and stop[0] == "0":
        return stages, (x_l0[0], [x_l0[1](b) for b in range(B)])

    wq, wk = (w1[:, i:i + 512].rearrange("p (c n) -> p c n", c=KC) for i in (0, 512))
    wv = w1[:, 1024:1280].rearrange("p (c n) -> p c n", c=KC)
    wo = w1[:, 1280:1792].rearrange("p (c n) -> p c n", c=KC)
    t1 = NormT(g, "transpose_l1", g.hT, x_l0, l0_end)
    p1 = Project(g, "l1_p", t1.drained(), l1_loads.done(), g.hT, g.cT, wq, wk, wv, col("l1_bq"),
                 col("l1_bk"), row("l1_bv"), 1, keys_ahead=True)
    a1 = SmallHeads(g, "l1_a", p1, 8, 8 ** -0.5, False, l1_loads.done())
    o1 = OutProject(g, "l1_o", a1.drained(), 8, wo, row("l1_bo"), t1.read_x(), [])
    n1 = NormRows(g, "l1_n", by_batch(o1.x), 1e-6, row("l1_gamma"), row("l1_beta"))
    split = SplitContext(g, [(l0.acc_done, 64), (l0.f_x, 4)])
    keys1 = KeysAhead(p1, l1_loads.done() + [(l0.f_xc, 4)])
    t2 = NormT(g, "l2_t1", g.hT, by_batch(n1.x), o1.drained(), (col("l2_ln1_scale"), col("l2_ln1_offset")),
               True)
    a2 = CrossAttention(g, "l2_a1", 0, t2.drained() + split.drained(), t2.read_x(), row("l2_bo1"),
                        [(l0.acc_done, 64)], [])
    keys2 = KeysAhead(a2, o1.drained() + [(a1.keys, a1.N)] + split.drained())
    p1.half_prev = t1.drained(B // 2)
    stages += [keys1, t1, split, FirstPair(a2), p1, BiasAhead(o1), a1, o1, keys2, n1]
    if stop and stop[0] == "1":
        return stages, (n1.x, list(range(1, B + 1)))

    masks = Loads(g, "l3_masks", [(g.mask[:, 0, :], ins["mask1"])], a1.drained())
    t3 = NormT(g, "l2_t2", g.hT, by_batch(a2.x), a2.drained(), (col("l2_ln2_scale"), col("l2_ln2_offset")),
               True)
    a3 = CrossAttention(g, "l2_a2", 1, t3.drained(), t3.read_x(), row("l2_bo2"),
                        [(a2.v_ready, 64)], [(a2.acc_done, 64)])
    t4 = NormT(g, "l2_t3", g.hT, by_batch(a3.x), a3.drained(),
               (col("l2_ln_mlp_scale"), col("l2_ln_mlp_offset")))
    m2 = Mlp(g, "l2_m", t4.drained(), ACT.Gelu, col("l2_b_fc1"), row("l2_b_fc2"), t4.read_x(),
             ("l2_w1", "l2_w2"), o1.drained())
    keys3 = KeysAhead(a3, [(a2.s_free, 16 * NPAIR)])
    a2.half_prev, a3.half_prev, m2.half_prev = (
        t.drained(B // 2) for t in (t2, t3, t4))
    stages += [masks, t2, MlpLoads(m2), a2, FirstPair(a3), keys3, t3, a3, t4, m2]
    if stop and stop[0] == "2":
        return stages, (m2.x, list(range(1, B + 1)))

    wa = g.wA[:, :]
    wc = g.wC[:, :]
    s_loads = Loads(g, "l3_self", [(wa, ins["l3_self"])], [(a3.acc_done, 64)])
    c_loads = Loads(g, "l3_cross", [(wc, ins["l3_cross"])])
    am1 = AdditiveMask(g, "l3_self", masks.done(), [])
    three = lambda w, n: w[:, 0:KC * n].rearrange("p (c n) -> p c n", c=KC)
    wqkv, wao = three(wa, 3 * D), wa[:, 1536:2048].rearrange("p (c n) -> p c n", c=KC)
    wq3, wkv3 = three(wc, D), wc[:, 512:1536].rearrange("p (c n) -> p c n", c=KC)
    wco = wc[:, 1536:2048].rearrange("p (c n) -> p c n", c=KC)
    t5 = NormT(g, "l3_t1", g.hT, by_batch(m2.x), m2.drained(), (col("l3_ln1_s"), col("l3_ln1_b")))
    p5 = Project(g, "l3_p1", t5.drained(), s_loads.done(), g.hT, g.hT, wqkv[:, :, 0:D],
                 wqkv[:, :, D:2 * D], wqkv[:, :, 2 * D:3 * D], col("l3_bq"), col("l3_bk"),
                 row("l3_bv"), 4)
    a5 = SmallHeads(g, "l3_a1", p5, 16, 0.25, True, masks.done() + am1.done())
    a5.one_mask = True
    o5 = OutProject(g, "l3_o1", a5.drained(), 16, wao, row("l3_b_ao"), t5.read_x(), [])
    masks2 = Loads(g, "l3_masks2", [(g.mask[:, :, :], ins["mask2"])], a5.drained())
    am2 = AdditiveMask(g, "l3_cross", masks2.done(), a5.drained())
    t6 = NormT(g, "l3_t2", g.hT, by_batch(o5.x), o5.drained(), (col("l3_ln2_s"), col("l3_ln2_b")))
    p6 = Project(g, "l3_p2", t6.drained(), c_loads.done(), g.hT, g.cT, wq3, wkv3[:, :, 0:D],
                 wkv3[:, :, D:2 * D], col("l3_bq2"), col("l3_bk2"), row("l3_bv2"), 4, keys_ahead=True)
    a6 = SmallHeads(g, "l3_a2", p6, 16, 0.25, True, masks2.done() + am2.done())
    o6 = OutProject(g, "l3_o2", a6.drained(), 16, wco, row("l3_b_co"), t6.read_x(), [])
    t7 = NormT(g, "l3_t3", g.hT, by_batch(o6.x), o6.drained(), (col("l3_ln3_s"), col("l3_ln3_b")))
    m3 = Mlp(g, "l3_m", t7.drained(), ACT.Gelu_apprx_tanh, col("l3_b1"), row("l3_b2"), t7.read_x(),
             ("l3_w1", "l3_w2"), [(m2.x, B)])
    keys6 = KeysAhead(p6, c_loads.done() + a5.drained() + [(a5.keys, a5.N), (o5.cx, B)])
    p5.half_prev, p6.half_prev, m3.half_prev = (
        t.drained(B // 2) for t in (t5, t6, t7))
    stages += [s_loads, c_loads, MlpLoads(m3), am1, t5, p5, BiasAhead(o5), a5, o5, keys6, masks2, am2,
               t6, p6,
               BiasAhead(o6), a6, o6, t7, m3]
    return stages, (m3.x, list(range(1, B + 1)))


class InputLoads:

    def __init__(self, stage):
        self.stage = stage

    def sp(self, e):
        self.stage.load_inputs(e)

    def pe(self, e):
        pass

    act = dve = pool = pe


class KeysAhead:

    def __init__(self, stage, prev):
        self.stage, self.prev = stage, prev

    def pe(self, e):
        for sem, value in self.prev:
            wait(e, sem, value)
        self.stage.project(e, 0)

    def act(self, e):
        self.stage.evacuate(e, 0)

    def pool(self, e):
        pass

    dve = sp = pool


class BiasAhead:

    def __init__(self, stage):
        self.stage = stage

    def pool(self, e):
        self.stage.add_bias(e)

    def pe(self, e):
        pass

    act = dve = sp = pe


class FirstPair:

    def __init__(self, stage):
        self.stage = stage

    def sp(self, e):
        self.stage.load_first(e)

    def pool(self, e):
        self.stage.prepare(e, 0)

    def pe(self, e):
        pass

    act = dve = pe


class MlpLoads:

    def __init__(self, mlp):
        self.mlp = mlp

    def sp(self, e):
        self.mlp.load(e)

    def pe(self, e):
        pass

    act = dve = pool = pe


def layout(a):
    f = {k: np.asarray(v) for k, v in a.items()}
    c = np.ascontiguousarray
    out = {}
    out["x_dbl"] = c(f["x"].transpose(1, 0, 2).reshape(P, B * D))
    out["ctx_dbl"] = c(f["ctx_2048"].transpose(1, 0, 2).reshape(P, B * D))
    out["ctxT"] = c(f["ctx_2048"].reshape(T, KC, P).transpose(2, 1, 0))
    w = np.stack([f["L0_xattn_Wqkv0"], f["L0_xattn_Winj0"], f["L0_xattn_Wqkv1"], f["L0_xattn_Winj1"]])
    w = w.reshape(4, 3, NPAIR, P, P).transpose(2, 4, 1, 0, 3).reshape(NPAIR, P, 12 * P)
    rwb = f["L0_xattn_r_w_bias"].reshape(NPAIR, P, 1)
    out["l0_w"] = c(np.concatenate([w, rwb], axis=2))
    out["l0_wo"] = c(f["L0_xattn_Wo"].reshape(P, NPAIR, P).transpose(1, 2, 0))
    tiles = lambda w: w.reshape(-1, P, w.shape[1]).transpose(1, 0, 2)
    flat = lambda w: w.reshape(P, -1)
    wk = np.broadcast_to(f["L1_xattn_Wk"].reshape(D, 8, 1, 8), (D, 8, 4, 8)).reshape(D, D)
    bk = np.broadcast_to(f["L1_xattn_bk"].reshape(8, 1, 8), (8, 4, 8)).reshape(D)
    wv = np.concatenate([f["L1_xattn_Wv"], np.zeros((D, 64), np.float32)], axis=1)
    out["l1_w"] = c(np.concatenate([flat(tiles(f["L1_xattn_Wq"])), flat(tiles(wk)), flat(tiles(wv)),
                                    flat(tiles(f["L1_xattn_Wo"]))], axis=1))
    w, wo, rows = [], [], []
    for i in "12":
        n = lambda name: f[f"L2_xattn_{name}{i}"]
        m = np.stack([n("wq"), n("wk"), n("wv")]).reshape(3, KC, P, NPAIR, D)
        m = m.transpose(3, 2, 0, 1, 4).reshape(NPAIR, P, 3 * KC * D)
        bias = np.stack([n(k).reshape(NPAIR, 2, P) for k in ("bq", "bk", "bias_k")])
        w.append(np.concatenate([m, bias.transpose(1, 3, 0, 2).reshape(NPAIR, P, 6)], axis=2))
        m = n("wo").reshape(NPAIR, 2, P, D).transpose(0, 2, 1, 3).reshape(NPAIR, P, 2 * D)
        wo.append(np.concatenate([m, n("bias_v").reshape(NPAIR, 2, P).transpose(0, 2, 1)], axis=2))
        rows.append(np.stack([n("bv").reshape(NPAIR, D), n("bias_v").reshape(NPAIR, D)], axis=1)
                    .reshape(NPAIR, 2 * D))
    for i in range(2):
        out[f"l2_w_{i}"], out[f"l2_wo_{i}"], out[f"l2_bv_{i}"] = c(w[i]), c(wo[i]), c(rows[i])
    out["l2_w1"], out["l2_w2"] = c(tiles(f["L2_xattn_w_fc1"])), c(tiles(f["L2_xattn_w_fc2"]))
    out["l3_self"] = c(np.concatenate([flat(tiles(f["L3_xattn_w_qkv"])),
                                       flat(tiles(f["L3_xattn_w_ao"]))], axis=1))
    out["l3_cross"] = c(np.concatenate([flat(tiles(f["L3_xattn_w_q"])), flat(tiles(f["L3_xattn_w_kv"])),
                                        flat(tiles(f["L3_xattn_w_co"]))], axis=1))
    out["l3_w1"], out["l3_w2"] = c(tiles(f["L3_xattn_w1"])), c(tiles(f["L3_xattn_w2"]))
    out["mask0"] = c(f["mask_Bx1xSxS2_ff0"][:, 0].transpose(1, 0, 2))
    out["mask1"] = c(f["mask_1x1xSxS2_fc1"][0, 0])
    out["mask2"] = c(f["mask_Bx1xSxS2_ff1"][:, 0].transpose(1, 0, 2))
    b_qkv, b_kv = f["L3_xattn_b_qkv"], f["L3_xattn_b_kv"]
    rows = {"l1_bv": np.concatenate([f["L1_xattn_bv"], np.zeros(D - 64, np.float32)]),
            "l3_bv": b_qkv[2 * D:], "l3_bv2": b_kv[D:]}
    cols = {"l1_bk": bk, "l3_bq": b_qkv[0:D], "l3_bk": b_qkv[D:2 * D], "l3_bq2": f["L3_xattn_b_q"],
            "l3_bk2": b_kv[0:D]}
    named = lambda name: f[name[0:2].upper() + "_xattn" + name[2:]]
    out["rows"] = c(np.concatenate([rows[n] if n in rows else named(n) for n in ROWS]).reshape(1, -1))
    out["cols"] = c(np.concatenate([(cols[n] if n in cols else named(n)).reshape(-1, P).T
                                    for n in COLS], axis=1))
    row = np.arange(P)[:, None]
    out["consts"] = np.concatenate([
        np.eye(P, dtype=np.float32), np.full((P, P), 1.0 / P, np.float32),
        (row // 8 == np.arange(16)[None, :]).astype(np.float32),
        (row // 16 == np.arange(8)[None, :]).astype(np.float32)], axis=1)
    return out


def kernel(**inputs):
    import concourse.bacc as bacc
    from concourse.bass_utils import run_bass_kernel_spmd

    nc = bacc.Bacc("TRN2", target_bir_lowering=False, num_devices=1)
    arrays = layout(inputs)
    ins = {k: nc.dram_tensor("in_" + k, a.shape, F32, kind="ExternalInput").ap() for k, a in arrays.items()}
    out = nc.dram_tensor("out", (B, P, D), F32, kind="ExternalOutput").ap()
    build_program(nc, ins, out)
    r = run_bass_kernel_spmd(nc, [{"in_" + k: a for k, a in arrays.items()}], core_ids=[0])
    return r.results[0]["out"]
```
